# Optimizing a Trainium2 kernel written in Bass

```python
import numpy as np
import jax
import jax.numpy as jnp

def _softmax(x, axis=-1):
    return jax.nn.softmax(x, axis=axis)

def _gelu(x):
    return jax.nn.gelu(x, approximate=True)

def _silu(x):
    return jax.nn.silu(x)

def _sigmoid(x):
    return jax.nn.sigmoid(x)

def _layernorm(x, axis=-1, eps=1e-05):
    m = jnp.mean(x, axis=axis, keepdims=True)
    v = jnp.var(x, axis=axis, keepdims=True)
    return (x - m) / jnp.sqrt(v + eps)

def _scatter_add(tgt, idx, src, axis=0):
    return tgt.at[idx].add(src)

def _segment_sum(src, seg, n):
    return jax.ops.segment_sum(src, seg, n)
kernel_name = 'mk_perceiver_d1_seqx_r2_84c7b0'

def setup_inputs(seed: int=0):
    np.random.seed(seed)
    _w = jnp.asarray

    def _rec_inputs():
        import jax
        import jax.numpy as jnp
        _rk = jax.random.key(seed)
        x = -0.0002928 + 1 * jax.random.normal(jax.random.fold_in(_rk, 1), (1, 256, 512), jnp.float32)
        _lenS = 256 - jax.random.randint(jax.random.fold_in(_rk, 7), (1,), 0, max(1, 256 // 4) + 1, jnp.int32)
        _lenS2 = 25088 - jax.random.randint(jax.random.fold_in(_rk, 8), (1,), 0, max(1, 25088 // 4) + 1, jnp.int32)
        _ctx_1024P = jax.random.normal(jax.random.fold_in(_rk, 11), (1, 16, 512), jnp.float32)
        _ctx_1024c = jax.random.dirichlet(jax.random.fold_in(_rk, 511), 0.3 * jnp.ones((16,), jnp.float32), (1, 25088))
        _ctx_1024t = jnp.einsum('bsk,bkd->bsd', _ctx_1024c, _ctx_1024P)
        _ctx_1024t = _ctx_1024t * jax.lax.rsqrt(jnp.mean(jnp.square(_ctx_1024t)) + 1e-12) * 0.953939
        ctx_1024 = -1.39393e-06 + 0.999914 * (_ctx_1024t + 0.3 * jax.random.normal(jax.random.fold_in(_rk, 611), (1, 25088, 512), jnp.float32))
        _validS = jnp.arange(256)[None, :] < _lenS[:, None]
        _validS2 = jnp.arange(25088)[None, :] < _lenS2[:, None]
        _causal = jnp.tril(jnp.ones((256, 256), dtype=bool))
        mask_1x1xSxS2_ik0 = jnp.where(jnp.broadcast_to(_validS2[0:1, None, None, :], (1, 1, 256, 25088)), 0, 1).astype(jnp.int32)
        return (x, ctx_1024, mask_1x1xSxS2_ik0)
    x, ctx_1024, mask_1x1xSxS2_ik0 = _rec_inputs()

    def _L0_xattn_setup():
        import jax, jax.numpy as jnp
        import numpy as np
        B, S, D, H = (2, 1024, 512, 16)
        HD = D // H
        key = jax.random.key(seed)
        ks = jax.random.split(key, 12)
        sc = 0.02
        inp = {'q': jax.random.normal(ks[0], (B, S, D), jnp.float32), 'k': jax.random.normal(ks[1], (B, S, D), jnp.float32), 'v': jax.random.normal(ks[2], (B, S, D), jnp.float32), 'mask': jnp.tril(jnp.ones((S, S), jnp.int32))[None, None], 'Wq': jax.random.normal(ks[3], (D, D), jnp.float32) * sc, 'bq': jnp.zeros((D,), jnp.float32), 'Wk': jax.random.normal(ks[4], (D, D), jnp.float32) * sc, 'bk': jnp.zeros((D,), jnp.float32), 'Wv': jax.random.normal(ks[5], (D, D), jnp.float32) * sc, 'bv': jnp.zeros((D,), jnp.float32), 'Wf': jax.random.normal(ks[6], (D, D), jnp.float32) * sc, 'bf': jnp.zeros((D,), jnp.float32)}
        return inp
    _L0_xattn_all = _L0_xattn_setup()
    _L0_xattn_in = {k: v for k, v in _L0_xattn_all.items() if k in ('Wq', 'bq', 'Wk', 'bk', 'Wv', 'bv', 'Wf', 'bf')}
    del _L0_xattn_all

    def _L0_attn_setup():
        import jax, jax.numpy as jnp
        import numpy as np
        D_MODEL = 512
        NHEAD = 16
        HEAD_DIM = D_MODEL // NHEAD
        WINDOW = 128
        BATCH = 2
        SEQ = 2048

        def _sliding_window_attention(q, k, v, window):
            B, H, S, D = q.shape
            W = window
            nc = S // W
            qc = q.reshape(B, H, nc, W, D)
            kb = k.reshape(B, H, nc, W, D)
            vb = v.reshape(B, H, nc, W, D)
            kprev = jnp.pad(kb, ((0, 0), (0, 0), (1, 0), (0, 0), (0, 0)))[:, :, :-1]
            vprev = jnp.pad(vb, ((0, 0), (0, 0), (1, 0), (0, 0), (0, 0)))[:, :, :-1]
            k2 = jnp.concatenate([kprev, kb], axis=3)
            v2 = jnp.concatenate([vprev, vb], axis=3)
            scores = jnp.einsum('bhcid,bhcjd->bhcij', qc, k2) / jnp.sqrt(jnp.asarray(D, dtype=q.dtype))
            i = jnp.arange(W)[:, None]
            j = jnp.arange(2 * W)[None, :]
            band = (j >= i + 1) & (j <= i + W)
            c = jnp.arange(nc)[:, None, None]
            valid = band[None] & ((c > 0) | (j[None] >= W))
            neg_inf = jnp.asarray(-jnp.inf, dtype=scores.dtype)
            scores = jnp.where(valid[None, None], scores, neg_inf)
            attn = jax.nn.softmax(scores, axis=-1)
            out = jnp.einsum('bhcij,bhcjd->bhcid', attn, v2)
            return out.reshape(B, H, S, D)
        key = jax.random.key(seed)
        kx, kq, kk, kv, ko = jax.random.split(key, 5)
        scale = 0.02
        return {'x': jax.random.normal(kx, (BATCH, SEQ, D_MODEL), dtype=jnp.float32), 'Wq': jax.random.normal(kq, (D_MODEL, D_MODEL), dtype=jnp.float32) * scale, 'Wk': jax.random.normal(kk, (D_MODEL, D_MODEL), dtype=jnp.float32) * scale, 'Wv': jax.random.normal(kv, (D_MODEL, D_MODEL), dtype=jnp.float32) * scale, 'Wo': jax.random.normal(ko, (D_MODEL, D_MODEL), dtype=jnp.float32) * scale}
    _L0_attn_all = _L0_attn_setup()
    _L0_attn_in = {k: v for k, v in _L0_attn_all.items() if k in ('Wq', 'Wk', 'Wv', 'Wo')}
    del _L0_attn_all

    def _L0_ffn_setup():
        import jax, jax.numpy as jnp
        import numpy as np
        E = 8
        K = 2
        B, S, H = (4, 1024, 512)
        key = jax.random.key(seed)
        k1, k2, k3 = jax.random.split(key, 3)
        hidden_states = jax.random.normal(k1, (B, S, H), dtype=jnp.float32)
        weight = jax.random.normal(k2, (E, H, H), dtype=jnp.float32) * 0.02
        bias = jnp.zeros((E, H), dtype=jnp.float32)
        router_weight = jax.random.normal(k3, (E, H), dtype=jnp.float32) * 0.01
        router_bias = jnp.zeros((E,), dtype=jnp.float32)
        return {'hidden_states': hidden_states, 'weight': weight, 'bias': bias, 'router_weight': router_weight, 'router_bias': router_bias}
    _L0_ffn_all = _L0_ffn_setup()
    _L0_ffn_in = {k: v for k, v in _L0_ffn_all.items() if k in ('weight', 'bias', 'router_weight', 'router_bias')}
    del _L0_ffn_all
    return {'x': x, 'ctx_1024': ctx_1024, 'mask_1x1xSxS2_ik0': mask_1x1xSxS2_ik0, 'L0_xattn_Wq': _L0_xattn_in['Wq'], 'L0_xattn_bq': _L0_xattn_in['bq'], 'L0_xattn_Wk': _L0_xattn_in['Wk'], 'L0_xattn_bk': _L0_xattn_in['bk'], 'L0_xattn_Wv': _L0_xattn_in['Wv'], 'L0_xattn_bv': _L0_xattn_in['bv'], 'L0_xattn_Wf': _L0_xattn_in['Wf'], 'L0_xattn_bf': _L0_xattn_in['bf'], 'L0_attn_Wq': _L0_attn_in['Wq'], 'L0_attn_Wk': _L0_attn_in['Wk'], 'L0_attn_Wv': _L0_attn_in['Wv'], 'L0_attn_Wo': _L0_attn_in['Wo'], 'L0_ffn_weight': _L0_ffn_in['weight'], 'L0_ffn_bias': _L0_ffn_in['bias'], 'L0_ffn_router_weight': _L0_ffn_in['router_weight'], 'L0_ffn_router_bias': _L0_ffn_in['router_bias']}

def reference(x, ctx_1024, mask_1x1xSxS2_ik0, L0_xattn_Wq, L0_xattn_bq, L0_xattn_Wk, L0_xattn_bk, L0_xattn_Wv, L0_xattn_bv, L0_xattn_Wf, L0_xattn_bf, L0_attn_Wq, L0_attn_Wk, L0_attn_Wv, L0_attn_Wo, L0_ffn_weight, L0_ffn_bias, L0_ffn_router_weight, L0_ffn_router_bias):
    import jax
    import jax.numpy as jnp

    def _L0_xattn_ref(q, k, v, mask, Wq, bq, Wk, bk, Wv, bv, Wf, bf):
        import jax, jax.numpy as jnp
        import numpy as np
        B, S, D, H = (2, 1024, 512, 16)
        HD = D // H
        b = q.shape[0]
        qh = (q @ Wq.T + bq).reshape(b, -1, H, HD).transpose(0, 2, 1, 3)
        kh = (k @ Wk.T + bk).reshape(b, -1, H, HD).transpose(0, 2, 1, 3)
        vh = (v @ Wv.T + bv).reshape(b, -1, H, HD).transpose(0, 2, 1, 3)
        scores = jnp.einsum('bhqd,bhkd->bhqk', qh, kh) / jnp.sqrt(jnp.float32(HD))
        scores = jnp.where(mask == 0, jnp.float32(-1000000000.0), scores)
        attn = jax.nn.softmax(scores, axis=-1)
        x = jnp.einsum('bhqk,bhkd->bhqd', attn, vh)
        x = x.transpose(0, 2, 1, 3).reshape(b, -1, D)
        return x @ Wf.T + bf

    def _L0_attn_ref(x, Wq, Wk, Wv, Wo):
        import jax, jax.numpy as jnp
        import numpy as np
        D_MODEL = 512
        NHEAD = 16
        HEAD_DIM = D_MODEL // NHEAD
        WINDOW = 128
        BATCH = 2
        SEQ = 2048

        def _sliding_window_attention(q, k, v, window):
            B, H, S, D = q.shape
            W = window
            nc = S // W
            qc = q.reshape(B, H, nc, W, D)
            kb = k.reshape(B, H, nc, W, D)
            vb = v.reshape(B, H, nc, W, D)
            kprev = jnp.pad(kb, ((0, 0), (0, 0), (1, 0), (0, 0), (0, 0)))[:, :, :-1]
            vprev = jnp.pad(vb, ((0, 0), (0, 0), (1, 0), (0, 0), (0, 0)))[:, :, :-1]
            k2 = jnp.concatenate([kprev, kb], axis=3)
            v2 = jnp.concatenate([vprev, vb], axis=3)
            scores = jnp.einsum('bhcid,bhcjd->bhcij', qc, k2) / jnp.sqrt(jnp.asarray(D, dtype=q.dtype))
            i = jnp.arange(W)[:, None]
            j = jnp.arange(2 * W)[None, :]
            band = (j >= i + 1) & (j <= i + W)
            c = jnp.arange(nc)[:, None, None]
            valid = band[None] & ((c > 0) | (j[None] >= W))
            neg_inf = jnp.asarray(-jnp.inf, dtype=scores.dtype)
            scores = jnp.where(valid[None, None], scores, neg_inf)
            attn = jax.nn.softmax(scores, axis=-1)
            out = jnp.einsum('bhcij,bhcjd->bhcid', attn, v2)
            return out.reshape(B, H, S, D)
        B, S, E = x.shape
        q = (x @ Wq.T).reshape(B, S, NHEAD, HEAD_DIM).transpose(0, 2, 1, 3)
        k = (x @ Wk.T).reshape(B, S, NHEAD, HEAD_DIM).transpose(0, 2, 1, 3)
        v = (x @ Wv.T).reshape(B, S, NHEAD, HEAD_DIM).transpose(0, 2, 1, 3)
        attn_out = _sliding_window_attention(q, k, v, WINDOW)
        attn_out = attn_out.transpose(0, 2, 1, 3).reshape(B, S, E)
        return attn_out @ Wo.T

    def _L0_ffn_ref(hidden_states, weight, bias, router_weight, router_bias):
        import jax, jax.numpy as jnp
        import numpy as np
        E = 8
        K = 2
        B, S, H = (4, 1024, 512)
        b, s, h = hidden_states.shape
        flat = hidden_states.reshape(b * s, h)
        logits = flat @ router_weight.T + router_bias
        scores = jax.nn.softmax(logits, axis=-1)
        _, topk_idx = jax.lax.top_k(scores, K)
        y = jnp.einsum('th,ehk->tek', flat, weight) + bias[None]
        sel = jnp.take_along_axis(y, topk_idx[:, :, None], axis=1)
        out = sel.sum(axis=1).reshape(b, s, h)
        return out
    x = x + _L0_xattn_ref(_layernorm(x, axis=-1), ctx_1024, ctx_1024, mask_1x1xSxS2_ik0, L0_xattn_Wq, L0_xattn_bq, L0_xattn_Wk, L0_xattn_bk, L0_xattn_Wv, L0_xattn_bv, L0_xattn_Wf, L0_xattn_bf)
    x = x + _L0_attn_ref(_layernorm(x, axis=-1), L0_attn_Wq, L0_attn_Wk, L0_attn_Wv, L0_attn_Wo)
    x = x + _L0_ffn_ref(_layernorm(x, axis=-1), L0_ffn_weight, L0_ffn_bias, L0_ffn_router_weight, L0_ffn_router_bias)
    return x

_drawn_inputs = setup_inputs


def setup_inputs(seed=0):
    import zlib

    import numpy as np

    out = dict(_drawn_inputs(seed))
    spreads = {'L0_xattn_bq': (0.0, 0.1),
     'L0_xattn_bk': (0.0, 0.1),
     'L0_xattn_bv': (0.0, 0.1),
     'L0_xattn_bf': (0.0, 0.1),
     'L0_ffn_bias': (0.0, 0.1),
     'L0_ffn_router_bias': (0.0, 0.1)}
    factors = {}
    for name, (base, spread) in spreads.items():
        noise = np.random.default_rng([zlib.crc32(name.encode()), seed]).standard_normal(out[name].shape)
        drawn = base * np.exp(spread * noise) if base else spread * noise
        out[name] = jnp.asarray(drawn.astype(out[name].dtype))
    for name, factor in factors.items():
        out[name] = (out[name] * factor).astype(out[name].dtype)
    return out
```

```python
from contextlib import ExitStack

import concourse.bass as bass
from concourse import mybir

F32 = mybir.dt.float32
BF16 = mybir.dt.bfloat16
I32 = mybir.dt.int32
ALU = mybir.AluOpType
ACT = mybir.ActivationFunctionType
AX = mybir.AxisListType

P = 128
BANK = 512
HEAD_DIM = 32
LN_EPS = 1e-5
MASKED = -1e30
LOWEST = -3e38
TOP_K = 2


def build_perceiver(nc, x, ctx, mask, wq, bq, wk, bk, wv, bv, wf, bf, awq, awk, awv, awo,
                    ffn_w, ffn_b, router_w, router_b, out):
    _, S, D = x.shape
    KEYS = ctx.shape[1]
    E = ffn_w.shape[0]
    H = D // HEAD_DIM
    SCALE = float(HEAD_DIM) ** -0.5
    QT = S // P
    C = D // P
    HG = P // HEAD_DIM
    CHUNK = BANK
    KT = CHUNK // P
    NCHUNK = KEYS // CHUNK
    GROUP = 7
    NGROUP = NCHUNK // GROUP
    PIECE = GROUP * CHUNK
    ACT_CHUNKS = 3
    assert QT == 2 and C == 4 and NGROUP * GROUP == NCHUNK and NCHUNK * CHUNK == KEYS and E == 8

    weights = [wq, wk, wv, wf, awq, awk, awv, awo]
    WQ, WK, WV, WF, AWQ, AWK, AWV, AWO = range(8)
    SLOT = [0, 1, 2, 3, 4, 5, 6, 0]
    NSTAGE = 3
    NSCAN = 3
    NPIECE = NGROUP * QT
    ORDER = [("w", 0), ("w", 1), ("s", 0), ("w", 2), ("s", 1), ("s", 2), ("w", 3), ("s", 3), ("s", 4),
             ("w", 4), ("s", 5), ("s", 6), ("w", 5), ("s", 7), ("s", 8), ("w", 6), ("s", 9), ("s", 10),
             ("w", 7), ("s", 11), ("s", 12), ("s", 13)]

    mask_q = mask.rearrange("a b (t p) k -> p (a b t) k", p=P)
    ctx_k = ctx.rearrange("a k d -> (a k) d")

    with ExitStack() as es:
        def sb(name, shape, dt=F32):
            return es.enter_context(nc.sbuf_tensor(name, shape, dt))

        def sem(name):
            return es.enter_context(nc.semaphore(name))

        ident = sb("ident", [P, P])
        ones_row = sb("ones_row", [1, P])
        bit_weight = sb("bit_weight", [1, GROUP])
        window = sb("window", [P, 2 * P])
        lower = sb("lower", [P, E, E])
        stage = sb("stage", [P, NSTAGE, C, D])
        wT = sb("wT", [P, 7, C, D])
        big = sb("big", [P, 11264])
        scan = big[:, 0:NSCAN * PIECE].bitcast(I32).rearrange("p (b k) -> p b k", b=NSCAN)
        pT = big[:, 0:8192].rearrange("p (b j k q) -> p b j k q", b=2, j=HG, k=KT)
        probs = big[:, 8192:11264].rearrange("p (b t k) -> p b t k", b=3, t=QT)
        pT2 = big[:, 0:H * 3 * P].rearrange("p (h k) -> p h k", h=H)
        probs2 = big[:, 8192:8192 + 3 * 3 * P].rearrange("p (b k) -> p b k", b=3)
        q_pad = sb("q_pad", [P, H, S])
        ctx_in = sb("ctx_in", [P, KT, D])
        ctxT = sb("ctxT", [P, C, CHUNK])
        kT = sb("kT", [P, C, CHUNK])
        v = sb("v", [P, KT, D])
        mask_in = sb("mask_in", [P, QT, CHUNK], I32)
        mask_add = sb("mask_add", [P, QT, CHUNK])
        oT = sb("oT", [P, C, S])
        res = sb("res", [P, QT, D])
        xn = mask_add
        xT = sb("xT", [P, C, S])
        wide = xT[:, :, :].rearrange("p c s -> p (c s)").rearrange("p (t h j) -> p t h j", t=QT, h=H)
        ln_stats = sb("ln_stats", [P, QT, 6])
        ln_mv = sb("ln_mv", [P, QT, 2])
        ln_rstd = sb("ln_rstd", [P, QT, 1])
        bias_rows = sb("bias_rows", [3 * C, P])
        bias_cols = sb("bias_cols", [P, 3, C])
        bf_row = sb("bf_row", [1, D])
        rb_row = sb("rb_row", [1, E])
        ffn_b_sb = sb("ffn_b_sb", [E, D])
        rw_rows = sb("rw_rows", [E, D])
        rwT = sb("rwT", [P, C, E])
        open_size = sb("open_size", [P, QT, NCHUNK])
        is_open = sb("is_open", [P, QT, NCHUNK])
        row_open = sb("row_open", [P, QT])
        row_shut = sb("row_shut", [P, QT])
        any_shut = sb("any_shut", [P, 1])
        chunk_need = sb("chunk_need", [P, NCHUNK])
        chunk_flag = sb("chunk_flag", [P, NCHUNK])
        chunk_bits = sb("chunk_bits", [1, NGROUP, GROUP])
        group_flag = sb("group_flag", [1, NGROUP])
        group_bits = sb("group_bits", [1, NGROUP])
        word_sums = sb("word_sums", [1, 1 + NGROUP])
        words = sb("words", [1, 1 + NGROUP], I32)
        gate = sb("gate", [P, QT, H])
        m_run = sb("m_run", [P, QT, H])
        m_new = sb("m_new", [P, QT, H])
        m_neg = sb("m_neg", [P, QT, H])
        m_diff = sb("m_diff", [P, QT, H])
        alpha = sb("alpha", [P, QT, H])
        chunk_sum = sb("chunk_sum", [P, QT, H])
        row_sum = sb("row_sum", [P, QT, H])
        row_inv = sb("row_inv", [P, QT, H])
        logit = sb("logit", [P, QT, E])
        r_max = sb("r_max", [P, QT, 1])
        score = sb("score", [P, QT, E])
        r_sum = sb("r_sum", [P, QT, 1])
        r_inv = sb("r_inv", [P, QT, 1])
        above = sb("above", [P, QT, E, E])
        tied = sb("tied", [P, QT, E, E])
        rank = sb("rank", [P, QT, E])
        chosen = sb("chosen", [P, QT, E])
        chosenT = sb("chosenT", [E, QT, P])
        ps = [es.enter_context(nc.psum_tensor(f"bank{i}", [P, BANK], F32)) for i in range(8)]

        x_loaded = sem("x_loaded")
        small_loaded = sem("small_loaded")
        stage_loaded = [sem(f"stage_loaded{i}") for i in range(NSTAGE)]
        scan_loaded = [sem(f"scan_loaded{i}") for i in range(NSCAN)]
        ctx_loaded = sem("ctx_loaded")
        mask_loaded = sem("mask_loaded")
        out_stored = sem("out_stored")
        pool_step = sem("pool_step")
        consts_ready = sem("consts_ready")
        dve_step = sem("dve_step")
        var_ready = sem("var_ready")
        std_ready = sem("std_ready")
        norm_ready = sem("norm_ready")
        tile_full = sem("tile_full")
        tile_act = sem("tile_act")
        tile_dve = sem("tile_dve")
        scan_act = sem("scan_act")
        scan_dve = sem("scan_dve")
        need_ready = sem("need_ready")
        flags_reduced = sem("flags_reduced")
        words_ready = sem("words_ready")
        ctx_turned = sem("ctx_turned")
        mask_used = sem("mask_used")
        ring_full = sem("ring_full")
        ring_act = sem("ring_act")
        ring_dve = sem("ring_dve")
        neg_ready = sem("neg_ready")
        probs_ready = sem("probs_ready")
        pT_full = sem("pT_full")
        pT_act = sem("pT_act")
        pT_dve = sem("pT_dve")
        pv_full = sem("pv_full")
        diff_ready = sem("diff_ready")
        alpha_ready = sem("alpha_ready")
        wide_ready = sem("wide_ready")
        alphaT_full = sem("alphaT_full")
        fold_step = sem("fold_step")
        neg2_ready = sem("neg2_ready")
        probs2_ready = sem("probs2_ready")
        pT2_full = sem("pT2_full")
        pT2_taken = sem("pT2_taken")
        pv2_full = sem("pv2_full")
        wide2_ready = sem("wide2_ready")
        wideT_full = sem("wideT_full")
        oT_ready = sem("oT_ready")
        proj_full = sem("proj_full")
        logits_full = sem("logits_full")
        shift_ready = sem("shift_ready")
        exp_ready = sem("exp_ready")
        chosen_ready = sem("chosen_ready")
        chosenT_full = sem("chosenT_full")
        chosenT_ready = sem("chosenT_ready")
        bias_full = sem("bias_full")
        y_full = sem("y_full")
        y_taken = sem("y_taken")
        out_ready = sem("out_ready")

        setup_tiles = [("x", 0), ("x", 1), ("small", 0)]
        setup_tiles += [("w", (0, o)) for o in range(C)] + [("q", g) for g in range(C)]
        for w in range(1, 8):
            setup_tiles += [("w", (w, o)) for o in range(C)]
        takers = ["dve" if kind in ("q", "small") or n % 2 else "act" for n, (kind, _) in enumerate(setup_tiles)]

        def taken(n, who_list=takers):
            who = who_list[n]
            return (tile_act if who == "act" else tile_dve), who_list[:n + 1].count(who)

        NSETUP = len(setup_tiles)
        w_tile = {a: n for n, (kind, a) in enumerate(setup_tiles) if kind == "w"}
        q_tile = [n for n, (kind, _) in enumerate(setup_tiles) if kind == "q"]

        late_takers = takers + ["act", "dve"] + ["act", "dve"] * 5 + ["dve"] * H + ["act", "dve"]
        LATE = NSETUP
        NLATE = len(late_takers) - LATE

        RING = 4
        NTILE = 3 * C + QT * H
        RING_DVE = 6 + QT * H
        NFULL = NTILE - KT
        FOLD = 10

        def ring_taken(n, d):
            if n < 3 * C:
                if n % 2:
                    return ring_dve, ONE + d * RING_DVE + n // 2 + 1
                return ring_act, d * 6 + n // 2 + 1
            return ring_dve, ONE + d * RING_DVE + 6 + n - 3 * C + 1

        def open_chunks(eng, body):
            done = eng.alloc_register("chunks_done")
            group_word = eng.alloc_register("group_word")
            chunk_word = eng.alloc_register("chunk_word")
            eng.reg_mov(done, 0)
            eng.wait_ge(words_ready, 1)
            eng.reg_mov(group_word, eng.value_load(words[0:1, 0:1], min_val=0, max_val=2 ** NGROUP - 1))
            with eng.Fori(0, NGROUP) as g:
                with eng.If((eng.snap(group_word) & 1) != 0):
                    eng.reg_mov(chunk_word, eng.value_load(words[0:1, bass.ds(g + 1, 1)], min_val=0,
                                                           max_val=2 ** GROUP - 1))
                    with eng.Fori(0, GROUP) as j:
                        with eng.If((eng.snap(chunk_word) & 1) != 0):
                            body(g * GROUP + j, eng.snap(done, min_val=0, max_val=NCHUNK - 1))
                            eng.reg_add(done, done, 1)
                        eng.reg_alu(chunk_word, chunk_word, 1, op=ALU.logical_shift_right)
                eng.reg_alu(group_word, group_word, 1, op=ALU.logical_shift_right)

        ONE = 1

        block = es.enter_context(nc.Block())

        @block.sync
        def _(sp):
            sp.dma_start(res[:, :, :], x.rearrange("a (t p) d -> p (a t) d", p=P)).then_inc(x_loaded, 16)
            for p in range(NPIECE):
                if p >= NSCAN:
                    sp.wait_ge(scan_act, p - NSCAN + 1)
                    sp.wait_ge(scan_dve, p - NSCAN + 1)
                g, t = p // QT, p % QT
                sp.dma_start(scan[:, p % NSCAN, :], mask_q[:, t, g * PIECE:(g + 1) * PIECE])\
                    .then_inc(scan_loaded[p % NSCAN], 16)

            def load_chunk(c, d):
                sp.wait_ge(mask_used, ONE + d)
                sp.wait_ge(ctx_turned, ONE + d * KT)
                sp.dma_start(ctx_in[:, :, :], ctx_k[bass.ds(c * CHUNK, CHUNK), :]
                             .rearrange("(t p) d -> p t d", p=P)).then_inc(ctx_loaded, 16)
                sp.dma_start(mask_in[:, :, :], mask_q[:, :, bass.ds(c * CHUNK, CHUNK)])\
                    .then_inc(mask_loaded, 16)

            open_chunks(sp, load_chunk)
            out_q = out.rearrange("a (t p) d -> p (a t) d", p=P)
            for t in range(QT):
                sp.wait_ge(out_ready, t + 1)
                sp.dma_start(out_q[:, t, :], res[:, t, :]).then_inc(out_stored, 16)
            sp.wait_ge(out_stored, 16 * QT)

        @block.gpsimd
        def _(pool):
            def load_weight(w):
                pool.dma_start(stage[:, w % NSTAGE, :, :], weights[w].rearrange("(o p) c -> p o c", p=P))\
                    .then_inc(stage_loaded[w % NSTAGE], 16)

            def load_expert(e):
                n = 8 + e
                pool.dma_start(stage[:, n % NSTAGE, :, :], ffn_w[e].rearrange("(c p) k -> p c k", p=P))\
                    .then_inc(stage_loaded[n % NSTAGE], 16)

            for w in range(NSTAGE):
                load_weight(w)
            nc.gpsimd.memset(ident[:, :], 0.0).then_inc(pool_step, 1)
            nc.gpsimd.memset(window[:, :], 0.0).then_inc(pool_step, 1)
            nc.gpsimd.memset(lower[:, :, :], 1.0).then_inc(pool_step, 1)
            pool.wait_ge(pool_step, 3)
            nc.gpsimd.affine_select(out=ident[:, :], in_=ident[:, :], compare_op=ALU.not_equal, fill=1.0,
                                    base=0, pattern=[[-1, P]], channel_multiplier=1).then_inc(consts_ready, 1)
            nc.gpsimd.affine_select(out=window[:, 0:P], in_=window[:, 0:P], compare_op=ALU.is_ge, fill=MASKED,
                                    base=-1, pattern=[[1, P]], channel_multiplier=-1).then_inc(consts_ready, 1)
            nc.gpsimd.affine_select(out=window[:, P:], in_=window[:, P:], compare_op=ALU.is_ge, fill=MASKED,
                                    base=0, pattern=[[-1, P]], channel_multiplier=1).then_inc(consts_ready, 1)
            nc.gpsimd.affine_select(out=lower[:, :, :], in_=lower[:, :, :], compare_op=ALU.is_ge, fill=0.0,
                                    base=-1, pattern=[[1, E], [-1, E]], channel_multiplier=0)\
                .then_inc(consts_ready, 1)
            nc.gpsimd.memset(ones_row[:, :], 1.0).then_inc(consts_ready, 1)
            for j in range(GROUP):
                nc.gpsimd.memset(bit_weight[:, j:j + 1], float(2 ** j)).then_inc(consts_ready, 1)
            nc.gpsimd.memset(q_pad[:, :, :], 0.0).then_inc(consts_ready, 1)
            nc.gpsimd.memset(oT[:, :, :], 0.0).then_inc(consts_ready, 1)
            nc.gpsimd.memset(m_run[:, :, :], LOWEST).then_inc(consts_ready, 1)
            nc.gpsimd.memset(row_sum[:, :, :], 0.0).then_inc(consts_ready, 1)
            for w in range(NSTAGE, 8):
                pool.wait_ge(tile_full, w_tile[(w - NSTAGE, C - 1)] + 1)
                load_weight(w)
            for e in range(NSTAGE):
                pool.wait_ge(tile_full, w_tile[(8 + e - NSTAGE, C - 1)] + 1)
                load_expert(e)
            pool.wait_ge(need_ready, 1)
            nc.gpsimd.partition_all_reduce(chunk_flag[:, :], chunk_need[:, :], P, bass.bass_isa.ReduceOp.max)\
                .then_inc(flags_reduced, 1)
            for e in range(NSTAGE, E):
                pool.wait_ge(y_full, QT * (e - NSTAGE + 1))
                load_expert(e)

        NCONST = 4 + 1 + GROUP + 4

        @block.tensor
        def _(pe):
            def transpose(o, i, n=P):
                return nc.tensor.transpose(o, i, ident[0:n, 0:n])

            def setup_tile(n):
                kind, a = setup_tiles[n]
                if n >= 8:
                    pe.wait_ge(*taken(n - 8))
                b = ps[n % 8]
                if kind == "x":
                    pe.wait_ge(norm_ready, a + 1)
                    for c in range(C):
                        last = transpose(b[:, c * P:(c + 1) * P], xn[:, a, c * P:(c + 1) * P])
                elif kind == "small":
                    pe.wait_ge(small_loaded, 16 * 7)
                    transpose(b[:, 0:3 * C], bias_rows[:, :], 3 * C)
                    for c in range(C):
                        last = transpose(b[:, 64 + c * E:64 + (c + 1) * E], rw_rows[:, c * P:(c + 1) * P], E)
                elif kind == "w":
                    w, o = a
                    pe.wait_ge(stage_loaded[w % NSTAGE], 16 * (w // NSTAGE + 1))
                    for c in range(C):
                        last = transpose(b[:, c * P:(c + 1) * P], stage[:, w % NSTAGE, o, c * P:(c + 1) * P])
                else:
                    if a == 0:
                        pe.wait_ge(*taken(0))
                        pe.wait_ge(*taken(1))
                        pe.wait_ge(*taken(w_tile[(WQ, C - 2)]))
                        pe.wait_ge(*taken(w_tile[(WQ, C - 1)]))
                    for c in range(C):
                        last = nc.tensor.matmul(b[:, 0:S], wT[:, SLOT[WQ], c, a * P:(a + 1) * P], xT[:, c, :],
                                                start=(c == 0), stop=(c == C - 1))
                last.then_inc(tile_full, 1)

            pe.sem_inc(ctx_turned, ONE)
            pe.sem_inc(pT_full, ONE)
            pe.wait_ge(consts_ready, NCONST)
            for n in range(NSETUP):
                setup_tile(n)
            pe.wait_ge(tile_act, takers.count("act"))
            pe.wait_ge(tile_dve, takers.count("dve"))

            def chunk(c, d):
                def ring(n, waits=()):
                    if n < RING:
                        pe.wait_ge(ring_dve, ONE + d * RING_DVE)
                    else:
                        pe.wait_ge(*ring_taken(n - RING, d))
                    for s, value in waits:
                        pe.wait_ge(s, value)
                    return ps[n % RING]

                for k in range(KT):
                    b = ring(k, [(ctx_loaded, d * 16 + 16)])
                    for cc in range(C):
                        last = transpose(b[:, cc * P:(cc + 1) * P], ctx_in[:, k, cc * P:(cc + 1) * P])
                    last.then_inc(ctx_turned, 1)
                for g in range(C):
                    b = ring(C + g, [ring_taken(n, d) for n in (2, 3)])
                    for cc in range(C):
                        last = nc.tensor.matmul(b[:, :], wT[:, SLOT[WK], cc, g * P:(g + 1) * P], ctxT[:, cc, :],
                                                start=(cc == 0), stop=(cc == C - 1))
                    last.then_inc(ring_full, 1)
                for k in range(KT):
                    b = ring(2 * C + k)
                    for cc in range(C):
                        last = nc.tensor.matmul(b[:, :], ctxT[:, cc, k * P:(k + 1) * P], wT[:, SLOT[WV], cc, :],
                                                start=(cc == 0), stop=(cc == C - 1))
                    last.then_inc(ring_full, 1)

                def scores(h):
                    for t in range(QT):
                        b = ring(3 * C + QT * h + t, [ring_taken(C + h // HG, d)])
                        nc.tensor.matmul(b[:, :], q_pad[:, h, t * P:(t + 1) * P], kT[:, h // HG, :],
                                         start=True, stop=True).then_inc(ring_full, 1)

                def turn_probs(h):
                    for t in range(QT):
                        m = QT * h + t
                        pe.wait_ge(probs_ready, d * QT * H + m + 1)
                        if h >= 1:
                            pe.wait_ge(pT_act if t == 0 else pT_dve, d * H + h)
                        elif t == 0:
                            pe.wait_ge(fold_step, ONE + d * FOLD)
                        b = ps[4 + m % 2]
                        for k in range(KT):
                            last = transpose(b[:, k * P:(k + 1) * P], probs[:, h % 3, t, k * P:(k + 1) * P])
                        last.then_inc(pT_full, 1)

                def weigh_values(g):
                    pe.wait_ge(pT_act, d * H + HG * (g + 1))
                    pe.wait_ge(pT_dve, d * H + HG * (g + 1))
                    if g == 0:
                        pe.wait_ge(*ring_taken(3 * C - 2, d))
                        pe.wait_ge(*ring_taken(3 * C - 1, d))
                    b = ps[6 + g // 2]
                    for k in range(KT):
                        for j in range(HG):
                            h = HG * g + j
                            rows = slice(j * HEAD_DIM, (j + 1) * HEAD_DIM)
                            last = nc.tensor.matmul(b[rows, (g % 2) * S:(g % 2 + 1) * S],
                                                    v[:, k, h * HEAD_DIM:(h + 1) * HEAD_DIM],
                                                    pT[:, g % 2, j, k, :], start=(k == 0), stop=(k == KT - 1),
                                                    tile_position=(0, j * HEAD_DIM))
                    last.then_inc(pv_full, 1)

                for i in range(H + 3):
                    if i < H:
                        scores(i)
                    if 2 <= i < H + 2:
                        turn_probs(i - 2)
                    if i >= 6 and (i - 6) % HG == 0:
                        weigh_values((i - 6) // HG)
                pe.wait_ge(wide_ready, d + 1)
                for g in range(C):
                    for t in range(QT):
                        at = (g % 2) * S + t * P
                        last = transpose(ps[4 + g // 2][:, at:at + P], wide[:, t, HG * g:HG * (g + 1), :])
                last.then_inc(alphaT_full, 1)

            open_chunks(pe, chunk)

            def spread(done_before):
                pe.wait_ge(wide2_ready, done_before)
                for g in range(C):
                    for t in range(QT):
                        at = (g % 2) * S + t * P
                        last = transpose(ps[4 + g // 2][:, at:at + P], wide[:, t, HG * g:HG * (g + 1), :])
                last.then_inc(wideT_full, 1)

            def project(w, n, bias_row=None):
                pe.wait_ge(oT_ready, n)
                for t in range(QT):
                    if bias_row is not None:
                        nc.tensor.matmul(ps[t][:, :], ones_row[:, :], bias_row[:, :], start=True, stop=False)
                    for g in range(C):
                        last = nc.tensor.matmul(ps[t][:, :], oT[:, g, t * P:(t + 1) * P], wT[:, SLOT[w], g, :],
                                                start=(g == 0 and bias_row is None), stop=(g == C - 1))
                    last.then_inc(proj_full, 1)

            spread(1)
            project(WF, 1, bf_row)

            def late(n):
                if n >= RING:
                    pe.wait_ge(*taken(LATE + n - RING, late_takers))
                return ps[n % RING]

            def late_wait(n):
                pe.wait_ge(*taken(LATE + n, late_takers))

            for t in range(QT):
                b = late(t)
                pe.wait_ge(norm_ready, QT + t + 1)
                for c in range(C):
                    last = transpose(b[:, c * P:(c + 1) * P], xn[:, t, c * P:(c + 1) * P])
                last.then_inc(tile_full, 1)
            late_wait(0)
            late_wait(1)
            for i, w in enumerate((AWQ, AWK)):
                for g in range(C):
                    b = late(QT + C * i + g)
                    for c in range(C):
                        last = nc.tensor.matmul(b[:, 0:S], wT[:, SLOT[w], c, g * P:(g + 1) * P], xT[:, c, :],
                                                start=(c == 0), stop=(c == C - 1))
                    last.then_inc(tile_full, 1)
            for t in range(QT):
                b = late(QT + 2 * C + t)
                for c in range(C):
                    last = nc.tensor.matmul(b[:, :], xT[:, c, t * P:(t + 1) * P], wT[:, SLOT[AWV], c, :],
                                            start=(c == 0), stop=(c == C - 1))
                last.then_inc(tile_full, 1)

            def scores2(h):
                b = late(2 * QT + 2 * C + h)
                if h % HG == 0:
                    late_wait(QT + h // HG)
                    late_wait(QT + C + h // HG)
                k2 = kT[:, h // HG, 0:S]
                nc.tensor.matmul(b[:, 0:P], q_pad[:, h, 0:P], k2[:, 0:P], start=True, stop=True)
                nc.tensor.matmul(b[:, P:3 * P], q_pad[:, h, P:2 * P], k2[:, :], start=True, stop=True)\
                    .then_inc(tile_full, 1)

            def turn_probs2(h):
                pe.wait_ge(probs2_ready, h + 1)
                if h >= 2:
                    pe.wait_ge(pT2_taken, h - 1)
                b = ps[4 + h % 2]
                for k in range(3):
                    last = transpose(b[:, k * P:(k + 1) * P], probs2[:, h % 3, k * P:(k + 1) * P])
                last.then_inc(pT2_full, 1)

            def weigh_values2(g):
                pe.wait_ge(pT2_taken, HG * (g + 1))
                if g == 0:
                    late_wait(QT + 2 * C)
                    late_wait(QT + 2 * C + 1)
                b = ps[6 + g // 2]
                at = (g % 2) * S
                for k, vt, col, first, final in ((0, 0, 0, True, True), (1, 0, P, True, False),
                                                 (2, 1, P, False, True)):
                    for j in range(HG):
                        h = HG * g + j
                        rows = slice(j * HEAD_DIM, (j + 1) * HEAD_DIM)
                        last = nc.tensor.matmul(b[rows, at + col:at + col + P],
                                                v[:, vt, h * HEAD_DIM:(h + 1) * HEAD_DIM],
                                                pT2[:, h, k * P:(k + 1) * P], start=first, stop=final,
                                                tile_position=(0, j * HEAD_DIM))
                last.then_inc(pv2_full, 1)

            for i in range(H + 3):
                if i < H:
                    scores2(i)
                if 2 <= i < H + 2:
                    turn_probs2(i - 2)
                if i >= 6 and (i - 6) % HG == 0:
                    weigh_values2((i - 6) // HG)
            spread(2)
            project(AWO, 2)

            for t in range(QT):
                pe.wait_ge(norm_ready, 2 * QT + t + 1)
                for c in range(C):
                    last = transpose(ps[2 + t][:, c * P:(c + 1) * P], xn[:, t, c * P:(c + 1) * P])
                last.then_inc(tile_full, 1)
            pe.wait_ge(*taken(LATE + NLATE - 2, late_takers))
            pe.wait_ge(*taken(LATE + NLATE - 1, late_takers))
            for t in range(QT):
                nc.tensor.matmul(ps[4][:, t * E:(t + 1) * E], ones_row[:, :], rb_row[:, :], start=True, stop=False)
                for c in range(C):
                    last = nc.tensor.matmul(ps[4][:, t * E:(t + 1) * E], xT[:, c, t * P:(t + 1) * P],
                                            rwT[:, c, :], start=False, stop=(c == C - 1))
            last.then_inc(logits_full, 1)

            def expert(n):
                e, t = n // QT, n % QT
                pe.wait_ge(stage_loaded[(8 + e) % NSTAGE], 16 * ((8 + e) // NSTAGE + 1))
                if n >= 4:
                    pe.wait_ge(y_taken, n - 3)
                b = ps[n % 4]
                for c in range(C):
                    last = nc.tensor.matmul(b[:, :], xT[:, c, t * P:(t + 1) * P], stage[:, (8 + e) % NSTAGE, c, :],
                                            start=(c == 0), stop=(c == C - 1))
                last.then_inc(y_full, 1)

            for n in range(4):
                expert(n)
            pe.wait_ge(chosen_ready, 1)
            for t in range(QT):
                last = transpose(ps[5][0:E, t * P:(t + 1) * P], chosen[:, t, :])
            last.then_inc(chosenT_full, 1)
            pe.wait_ge(chosenT_ready, 1)
            for t in range(QT):
                last = nc.tensor.matmul(ps[6 + t][:, :], chosenT[:, t, :], ffn_b_sb[:, :], start=True, stop=True)
            last.then_inc(bias_full, 1)
            for n in range(4, QT * E):
                expert(n)


        @block.scalar
        def _(act):
            for i, b in enumerate((bq, bk, bv)):
                act.dma_start(bias_rows[C * i:C * (i + 1), :], b.rearrange("(c p) -> c p", p=P))\
                    .then_inc(small_loaded, 16)
            act.dma_start(rw_rows[:, :], router_w).then_inc(small_loaded, 16)
            act.dma_start(bf_row[:, :], bf.rearrange("(a d) -> a d", a=1)).then_inc(small_loaded, 16)
            act.dma_start(rb_row[:, :], router_b.rearrange("(a d) -> a d", a=1)).then_inc(small_loaded, 16)
            act.dma_start(ffn_b_sb[:, :], ffn_b).then_inc(small_loaded, 16)

            def layer_norm_root(n):
                act.wait_ge(var_ready, n)
                nc.scalar.activation(ln_rstd[:, :, :], ln_rstd[:, :, :], ACT.Sqrt).then_inc(std_ready, 1)

            layer_norm_root(1)

            def take_setup(n):
                kind, a = setup_tiles[n]
                act.wait_ge(tile_full, n + 1)
                dst = xT[:, :, a * P:(a + 1) * P] if kind == "x" else None
                if kind == "w":
                    w, o = a
                    if w == AWO and o < 2:
                        act.wait_ge(tile_full, q_tile[-1] + 1)
                    dst = wT[:, SLOT[w], :, o * P:(o + 1) * P]
                nc.scalar.activation(dst, ps[n % 8][:, :].rearrange("p (c q) -> p c q", c=C), ACT.Copy)\
                    .then_inc(tile_act, 1)

            def scan_piece(p):
                g, t = p // QT, p % QT
                act.wait_ge(scan_loaded[p % NSCAN], 16 * (p // NSCAN + 1))
                for i in range(GROUP - ACT_CHUNKS, GROUP):
                    piece = scan[:, p % NSCAN, i * CHUNK:(i + 1) * CHUNK]
                    last = nc.scalar.activation(piece.bitcast(F32), piece, ACT.Abs,
                                                accum_out=open_size[:, t, g * GROUP + i:g * GROUP + i + 1])
                last.then_inc(scan_act, 1)

            for n in range(q_tile[0]):
                if n < w_tile[(0, 0)] and takers[n] == "act":
                    take_setup(n)
            for kind, i in ORDER:
                if kind == "s":
                    scan_piece(i)
                else:
                    for o in range(C):
                        if takers[w_tile[(i, o)]] == "act":
                            take_setup(w_tile[(i, o)])

            def chunk(c, d):
                for n in (0, 2):
                    act.wait_ge(ctx_turned, ONE + d * KT + n + 1)
                    nc.scalar.activation(ctxT[:, :, n * P:(n + 1) * P],
                                         ps[n % RING][:, :].rearrange("p (c k) -> p c k", c=C), ACT.Copy)\
                        .then_inc(ring_act, 1)
                for g in (0, 2):
                    act.wait_ge(ring_full, d * NFULL + g + 1)
                    nc.scalar.activation(kT[:, g, :], ps[(C + g) % RING][:, :], ACT.Identity,
                                         bias=bias_cols[:, 1, g:g + 1]).then_inc(ring_act, 1)
                for k in (0, 2):
                    act.wait_ge(ring_full, d * NFULL + C + k + 1)
                    nc.scalar.activation(v[:, k, :], ps[(2 * C + k) % RING][:, :], ACT.Copy).then_inc(ring_act, 1)
                for i in range(H + 2):
                    if i < H:
                        act.wait_ge(neg_ready, d * H + i + 1)
                        for t in range(QT):
                            nc.scalar.activation(probs[:, i % 3, t, :], probs[:, i % 3, t, :], ACT.Exp,
                                                 bias=m_neg[:, t, i:i + 1],
                                                 accum_out=chunk_sum[:, t, i:i + 1]).then_inc(probs_ready, 1)
                    if i >= 2:
                        h = i - 2
                        act.wait_ge(pT_full, ONE + d * QT * H + QT * h + 1)
                        if h % HG == 0 and h // HG >= 2:
                            act.wait_ge(pv_full, d * C + h // HG - 1)
                        nc.scalar.activation(pT[:, (h // HG) % 2, h % HG, :, 0:P],
                                             ps[4][:, :].rearrange("p (k q) -> p k q", k=KT), ACT.Copy)\
                            .then_inc(pT_act, 1)
                act.wait_ge(diff_ready, d + 1)
                nc.scalar.activation(alpha[:, :, :], m_diff[:, :, :], ACT.Exp).then_inc(alpha_ready, 1)

            open_chunks(act, chunk)

            layer_norm_root(2)
            act.wait_ge(tile_full, LATE + 1)
            nc.scalar.activation(xT[:, :, 0:P], ps[0][:, :].rearrange("p (c q) -> p c q", c=C), ACT.Copy)\
                .then_inc(tile_act, 1)
            for g in (0, 2):
                n = QT + g
                act.wait_ge(tile_full, LATE + n + 1)
                for j in range(HG):
                    rows = slice(j * HEAD_DIM, (j + 1) * HEAD_DIM)
                    last = nc.scalar.activation(q_pad[rows, HG * g + j, :], ps[n % RING][rows, 0:S], ACT.Copy,
                                                scale=SCALE)
                last.then_inc(tile_act, 1)
            for g in (0, 2):
                n = QT + C + g
                act.wait_ge(tile_full, LATE + n + 1)
                nc.scalar.activation(kT[:, g, 0:S], ps[n % RING][:, 0:S], ACT.Copy).then_inc(tile_act, 1)
            n = QT + 2 * C
            act.wait_ge(tile_full, LATE + n + 1)
            nc.scalar.activation(v[:, 0, :], ps[n % RING][:, :], ACT.Copy).then_inc(tile_act, 1)
            for i in range(H + 2):
                if i < H:
                    act.wait_ge(neg2_ready, i + 1)
                    nc.scalar.activation(probs2[:, i % 3, 0:P], probs2[:, i % 3, 0:P], ACT.Exp,
                                         bias=m_neg[:, 0, i:i + 1], accum_out=row_sum[:, 0, i:i + 1])
                    nc.scalar.activation(probs2[:, i % 3, P:], probs2[:, i % 3, P:], ACT.Exp,
                                         bias=m_neg[:, 1, i:i + 1], accum_out=row_sum[:, 1, i:i + 1])\
                        .then_inc(probs2_ready, 1)
                if i >= 2:
                    h = i - 2
                    act.wait_ge(pT2_full, h + 1)
                    nc.scalar.activation(pT2[:, h, :], ps[4 + h % 2][:, 0:3 * P], ACT.Copy).then_inc(pT2_taken, 1)

            layer_norm_root(3)
            act.wait_ge(tile_full, LATE + NLATE - 1)
            nc.scalar.activation(xT[:, :, 0:P], ps[2][:, :].rearrange("p (c q) -> p c q", c=C), ACT.Copy)\
                .then_inc(tile_act, 1)
            act.wait_ge(shift_ready, 1)
            nc.scalar.activation(score[:, :, :], logit[:, :, :], ACT.Exp).then_inc(exp_ready, 1)
            act.wait_ge(chosenT_full, 1)
            nc.scalar.activation(chosenT[:, :, :], ps[5][0:E, 0:QT * P].rearrange("e (t q) -> e t q", t=QT), ACT.Copy)\
                .then_inc(chosenT_ready, 1)

        @block.vector
        def _(dve):
            steps = [0]
            norms = [0]

            def link(ins):
                steps[0] += 1
                ins.then_inc(dve_step, 1)
                dve.wait_ge(dve_step, steps[0])

            def layer_norm():
                for t in range(QT):
                    last = nc.vector.bn_stats(ln_stats[:, t, :], res[:, t, :])
                link(last)
                for t in range(QT):
                    last = nc.vector.bn_aggr(ln_mv[:, t, :], ln_stats[:, t, :])
                link(last)
                nc.vector.tensor_scalar(ln_rstd[:, :, :], ln_mv[:, :, 1:2], LN_EPS, None, ALU.add)\
                    .then_inc(var_ready, 1)
                norms[0] += 1
                dve.wait_ge(std_ready, norms[0])
                link(nc.vector.reciprocal(ln_rstd[:, :, :], ln_rstd[:, :, :]))
                for t in range(QT):
                    nc.vector.tensor_scalar(xn[:, t, :], res[:, t, :], ln_mv[:, t, 0:1], ln_rstd[:, t, :],
                                            ALU.subtract, ALU.mult).then_inc(norm_ready, 1)

            def take_setup(n):
                kind, a = setup_tiles[n]
                dve.wait_ge(tile_full, n + 1)
                b = ps[n % 8]
                quarters = b[:, :].rearrange("p (c q) -> p c q", c=C)
                if kind == "x":
                    last = nc.vector.tensor_copy(xT[:, :, a * P:(a + 1) * P], quarters)
                elif kind == "w":
                    w, o = a
                    last = nc.vector.tensor_copy(wT[:, SLOT[w], :, o * P:(o + 1) * P], quarters)
                elif kind == "small":
                    link(nc.vector.tensor_copy(bias_cols[:, :, :], b[:, 0:3 * C].rearrange("p (i c) -> p i c", i=3)))
                    last = nc.vector.tensor_copy(rwT[:, :, :], b[:, 64:64 + C * E].rearrange("p (c e) -> p c e", c=C))
                else:
                    if a == 0:
                        dve.wait_ge(consts_ready, NCONST)
                    for j in range(HG):
                        rows = slice(j * HEAD_DIM, (j + 1) * HEAD_DIM)
                        last = nc.vector.tensor_scalar(q_pad[rows, HG * a + j, :], b[rows, 0:S],
                                                       bias_cols[rows, 0, a:a + 1], SCALE, ALU.add, ALU.mult)
                last.then_inc(tile_dve, 1)

            def scan_piece(p):
                g, t = p // QT, p % QT
                n = GROUP - ACT_CHUNKS
                dve.wait_ge(scan_loaded[p % NSCAN], 16 * (p // NSCAN + 1))
                nc.vector.tensor_reduce(open_size[:, t, g * GROUP:g * GROUP + n],
                                        scan[:, p % NSCAN, 0:n * CHUNK].rearrange("p (c k) -> p c k", c=n),
                                        AX.X, ALU.max, apply_absolute_value=True).then_inc(scan_dve, 1)

            for s in (mask_used, ring_dve, fold_step):
                dve.sem_inc(s, ONE)
            dve.wait_ge(x_loaded, 16)
            layer_norm()
            for n in range(3):
                if takers[n] == "dve":
                    take_setup(n)
            for kind, i in ORDER:
                if kind == "s":
                    scan_piece(i)
                else:
                    for o in range(C):
                        if takers[w_tile[(i, o)]] == "dve":
                            take_setup(w_tile[(i, o)])
                    if i == WQ:
                        for n in q_tile:
                            take_setup(n)

            dve.wait_ge(scan_act, NPIECE)
            dve.wait_ge(scan_dve, NPIECE)
            link(nc.vector.tensor_scalar(is_open[:, :, :], open_size[:, :, :], 0.0, None, ALU.is_gt))
            link(nc.vector.tensor_reduce(row_open[:, :], is_open[:, :, :], AX.X, ALU.max))
            link(nc.vector.tensor_scalar(row_shut[:, :], row_open[:, :], 0.0, None, ALU.is_equal))
            link(nc.vector.tensor_reduce(any_shut[:, :], row_shut[:, :], AX.X, ALU.max))
            nc.vector.scalar_tensor_tensor(out=chunk_need[:, :], in0=is_open[:, 0, :], scalar=any_shut[:, 0:1],
                                           in1=is_open[:, 1, :], op0=ALU.max, op1=ALU.max).then_inc(need_ready, 1)
            dve.wait_ge(flags_reduced, 1)
            flags = chunk_flag[0:1, :].rearrange("a (g j) -> a g j", g=NGROUP)
            nc.vector.tensor_tensor(chunk_bits[:, :, :], flags,
                                    bit_weight[:, :].unsqueeze(1).broadcast_to([1, NGROUP, GROUP]), ALU.mult)
            link(nc.vector.tensor_reduce(group_flag[:, :], flags, AX.X, ALU.max))
            link(nc.vector.tensor_tensor(group_bits[:, :], group_flag[:, :], bit_weight[:, 0:NGROUP], ALU.mult))
            nc.vector.tensor_reduce(word_sums[:, 0:1], group_bits[:, :], AX.X, ALU.add)
            link(nc.vector.tensor_reduce(word_sums[:, 1:1 + NGROUP], chunk_bits[:, :, :], AX.X, ALU.add))
            link(nc.vector.tensor_copy(words[:, :], word_sums[:, :]))
            dve.sem_inc(words_ready, 1)

            def chunk(c, d):
                dve.wait_ge(mask_loaded, d * 16 + 16)
                fold = [0]

                def fold_link(ins):
                    fold[0] += 1
                    ins.then_inc(fold_step, 1)
                    dve.wait_ge(fold_step, ONE + d * FOLD + fold[0])

                fold_link(nc.vector.tensor_scalar(mask_add[:, :, :], mask_in[:, :, :], 0.0, MASKED,
                                                  ALU.is_equal, ALU.mult))
                dve.sem_inc(mask_used, 1)
                for n in (1, 3):
                    dve.wait_ge(ctx_turned, ONE + d * KT + n + 1)
                    nc.vector.tensor_copy(ctxT[:, :, n * P:(n + 1) * P],
                                          ps[n % RING][:, :].rearrange("p (c k) -> p c k", c=C))\
                        .then_inc(ring_dve, 1)
                for g in (1, 3):
                    dve.wait_ge(ring_full, d * NFULL + g + 1)
                    nc.vector.tensor_scalar(kT[:, g, :], ps[(C + g) % RING][:, :], bias_cols[:, 1, g:g + 1], None,
                                            ALU.add).then_inc(ring_dve, 1)
                for k in (1, 3):
                    dve.wait_ge(ring_full, d * NFULL + C + k + 1)
                    nc.vector.tensor_copy(v[:, k, :], ps[(2 * C + k) % RING][:, :]).then_inc(ring_dve, 1)
                for i in range(H + 2):
                    if i < H:
                        if i >= 3:
                            dve.wait_ge(pT_full, ONE + d * QT * H + QT * (i - 2))
                        else:
                            dve.wait_ge(pT_full, ONE + d * QT * H)
                        for t in range(QT):
                            n = 3 * C + QT * i + t
                            dve.wait_ge(ring_full, d * NFULL + n - KT + 1)
                            nc.vector.memset(gate[:, t, i:i + 1], 0.0)
                            nc.vector.tensor_tensor_reduce(probs[:, i % 3, t, :], ps[n % RING][:, :], mask_add[:, t, :],
                                                           1.0, m_run[:, t, i:i + 1], ALU.add, ALU.max,
                                                           m_new[:, t, i:i + 1]).then_inc(ring_dve, 1)
                        dve.wait_ge(ring_dve, ONE + d * RING_DVE + 6 + QT * (i + 1))
                        nc.vector.tensor_scalar(m_neg[:, :, i:i + 1], m_new[:, :, i:i + 1], -1.0, None, ALU.mult)\
                            .then_inc(neg_ready, 1)
                    if i >= 2:
                        h = i - 2
                        dve.wait_ge(pT_full, ONE + d * QT * H + QT * h + 2)
                        if h % HG == 0 and h // HG >= 2:
                            dve.wait_ge(pv_full, d * C + h // HG - 1)
                        nc.vector.tensor_copy(pT[:, (h // HG) % 2, h % HG, :, P:2 * P],
                                              ps[5][:, :].rearrange("p (k q) -> p k q", k=KT)).then_inc(pT_dve, 1)
                dve.wait_ge(probs_ready, (d + 1) * QT * H)
                fold_link(nc.vector.tensor_tensor(m_diff[:, :, :], m_run[:, :, :], m_new[:, :, :], ALU.subtract))
                dve.sem_inc(diff_ready, 1)
                dve.wait_ge(alpha_ready, d + 1)
                fold_link(nc.vector.tensor_copy(wide[:, :, :, :],
                                                alpha[:, :, :].unsqueeze(3).broadcast_to([P, QT, H, HEAD_DIM])))
                dve.sem_inc(wide_ready, 1)
                fold_link(nc.vector.tensor_tensor(row_sum[:, :, :], row_sum[:, :, :], alpha[:, :, :], ALU.mult))
                fold_link(nc.vector.tensor_tensor(row_sum[:, :, :], row_sum[:, :, :], chunk_sum[:, :, :], ALU.add))
                fold_link(nc.vector.tensor_copy(m_run[:, :, :], m_new[:, :, :]))
                dve.wait_ge(alphaT_full, d + 1)
                dve.wait_ge(pv_full, (d + 1) * C)
                for b in range(2):
                    half = oT[:, 2 * b:2 * b + 2, :].rearrange("p g q -> p (g q)")
                    fold_link(nc.vector.tensor_tensor(half, half, ps[4 + b][:, :], ALU.mult))
                    fold_link(nc.vector.tensor_tensor(half, half, ps[6 + b][:, :], ALU.add))
                assert fold[0] == FOLD

            open_chunks(dve, chunk)

            def divide_and_spread(src_ready=None):
                link(nc.vector.reciprocal(row_inv[:, :, :], row_sum[:, :, :]))
                link(nc.vector.tensor_copy(wide[:, :, :, :],
                                           row_inv[:, :, :].unsqueeze(3).broadcast_to([P, QT, H, HEAD_DIM])))
                dve.sem_inc(wide2_ready, 1)

            divide_and_spread()
            dve.wait_ge(wideT_full, 1)
            for b in range(2):
                half = oT[:, 2 * b:2 * b + 2, :].rearrange("p g q -> p (g q)")
                link(nc.vector.tensor_tensor(half, half, ps[4 + b][:, :], ALU.mult))
            for g in range(C):
                link(nc.vector.tensor_scalar(oT[:, g, :], oT[:, g, :], bias_cols[:, 2, g:g + 1], None, ALU.add))
            dve.sem_inc(oT_ready, 1)

            def add_projection(n):
                for t in range(QT):
                    dve.wait_ge(proj_full, QT * n + t + 1)
                    link(nc.vector.tensor_tensor(res[:, t, :], res[:, t, :], ps[t][:, :], ALU.add))

            add_projection(0)
            layer_norm()

            def late_wait(n):
                dve.wait_ge(tile_full, LATE + n + 1)
                return ps[n % RING]

            b = late_wait(1)
            nc.vector.tensor_copy(xT[:, :, P:2 * P], b[:, :].rearrange("p (c q) -> p c q", c=C))\
                .then_inc(tile_dve, 1)
            for g in (1, 3):
                b = late_wait(QT + g)
                for j in range(HG):
                    rows = slice(j * HEAD_DIM, (j + 1) * HEAD_DIM)
                    last = nc.vector.tensor_scalar(q_pad[rows, HG * g + j, :], b[rows, 0:S], SCALE, None, ALU.mult)
                last.then_inc(tile_dve, 1)
            for g in (1, 3):
                b = late_wait(QT + C + g)
                nc.vector.tensor_copy(kT[:, g, 0:S], b[:, 0:S]).then_inc(tile_dve, 1)
            b = late_wait(QT + 2 * C + 1)
            nc.vector.tensor_copy(v[:, 1, :], b[:, :]).then_inc(tile_dve, 1)
            for h in range(H):
                b = late_wait(2 * QT + 2 * C + h)
                if h >= 3:
                    dve.wait_ge(pT2_full, h - 2)
                p2 = probs2[:, h % 3, :]
                nc.vector.tensor_tensor_reduce(p2[:, 0:P], b[:, 0:P], window[:, P:], 1.0, LOWEST, ALU.add, ALU.max,
                                               m_new[:, 0, h:h + 1])
                nc.vector.tensor_tensor_reduce(p2[:, P:], b[:, P:3 * P], window[:, :], 1.0, LOWEST, ALU.add, ALU.max,
                                               m_new[:, 1, h:h + 1]).then_inc(tile_dve, 1)
                dve.wait_ge(*taken(LATE + 2 * QT + 2 * C + h, late_takers))
                nc.vector.tensor_scalar(m_neg[:, :, h:h + 1], m_new[:, :, h:h + 1], -1.0, None, ALU.mult)\
                    .then_inc(neg2_ready, 1)
            dve.wait_ge(probs2_ready, H)
            divide_and_spread()
            for g in range(2):
                dve.wait_ge(pv2_full, 2 * g + 2)
                half = oT[:, 2 * g:2 * g + 2, :].rearrange("p g q -> p (g q)")
                link(nc.vector.tensor_copy(half, ps[6 + g][:, :]))
            dve.wait_ge(wideT_full, 2)
            for b in range(2):
                half = oT[:, 2 * b:2 * b + 2, :].rearrange("p g q -> p (g q)")
                link(nc.vector.tensor_tensor(half, half, ps[4 + b][:, :], ALU.mult))
            dve.sem_inc(oT_ready, 1)
            add_projection(1)
            layer_norm()

            dve.wait_ge(tile_full, LATE + NLATE)
            nc.vector.tensor_copy(xT[:, :, P:2 * P], ps[3][:, :].rearrange("p (c q) -> p c q", c=C))\
                .then_inc(tile_dve, 1)
            dve.wait_ge(logits_full, 1)
            logits = ps[4][:, 0:QT * E].rearrange("p (t e) -> p t e", t=QT)
            link(nc.vector.tensor_reduce(r_max[:, :, :], logits, AX.X, ALU.max))
            link(nc.vector.tensor_tensor(logit[:, :, :], logits, r_max[:, :, :].broadcast_to([P, QT, E]),
                                         ALU.subtract))
            dve.sem_inc(shift_ready, 1)
            dve.wait_ge(exp_ready, 1)
            link(nc.vector.tensor_reduce(r_sum[:, :, :], score[:, :, :], AX.X, ALU.add))
            link(nc.vector.reciprocal(r_inv[:, :, :], r_sum[:, :, :]))
            link(nc.vector.tensor_tensor(score[:, :, :], score[:, :, :], r_inv[:, :, :].broadcast_to([P, QT, E]),
                                         ALU.mult))
            for t in range(QT):
                other = score[:, t, :].unsqueeze(1).broadcast_to([P, E, E])
                own = score[:, t, :].unsqueeze(2).broadcast_to([P, E, E])
                nc.vector.tensor_tensor(above[:, t, :, :], other, own, ALU.is_gt)
                link(nc.vector.tensor_tensor(tied[:, t, :, :], other, own, ALU.is_equal))
                link(nc.vector.tensor_tensor(tied[:, t, :, :], tied[:, t, :, :], lower[:, :, :], ALU.mult))
                link(nc.vector.tensor_tensor(above[:, t, :, :], above[:, t, :, :], tied[:, t, :, :], ALU.add))
            link(nc.vector.tensor_reduce(rank[:, :, :], above[:, :, :, :], AX.X, ALU.add))
            link(nc.vector.tensor_scalar(chosen[:, :, :], rank[:, :, :], TOP_K - 0.5, None, ALU.is_lt))
            dve.sem_inc(chosen_ready, 1)

            dve.wait_ge(bias_full, 1)
            for t in range(QT):
                link(nc.vector.tensor_tensor(res[:, t, :], res[:, t, :], ps[6 + t][:, :], ALU.add))
            for n in range(QT * E):
                e, t = n // QT, n % QT
                dve.wait_ge(y_full, n + 1)
                if n >= QT:
                    dve.wait_ge(y_taken, n - QT + 1)
                nc.vector.scalar_tensor_tensor(out=res[:, t, :], in0=ps[n % 4][:, :], scalar=chosen[:, t, e:e + 1],
                                               in1=res[:, t, :], op0=ALU.mult, op1=ALU.add)\
                    .then_inc(y_taken, 1)
            for t in range(QT):
                dve.wait_ge(y_taken, QT * (E - 1) + t + 1)
                dve.sem_inc(out_ready, 1)


_INS = ['x', 'ctx_1024', 'mask_1x1xSxS2_ik0', 'L0_xattn_Wq', 'L0_xattn_bq', 'L0_xattn_Wk', 'L0_xattn_bk',
        'L0_xattn_Wv', 'L0_xattn_bv', 'L0_xattn_Wf', 'L0_xattn_bf', 'L0_attn_Wq', 'L0_attn_Wk', 'L0_attn_Wv',
        'L0_attn_Wo', 'L0_ffn_weight', 'L0_ffn_bias', 'L0_ffn_router_weight', 'L0_ffn_router_bias']


def kernel(**inputs):
    import numpy as np
    import concourse.bacc as bacc
    from concourse.bass_utils import run_bass_kernel_spmd

    nc = bacc.Bacc("TRN2", target_bir_lowering=False, num_devices=1)
    arrays, args = {}, []
    for name in _INS:
        a = np.ascontiguousarray(inputs[name])
        arrays[f"in_{name}"] = a
        args.append(nc.dram_tensor(f"in_{name}", a.shape, mybir.dt.from_np(a.dtype), kind="ExternalInput").ap())
    out = nc.dram_tensor("out_x", inputs['x'].shape, F32, kind="ExternalOutput").ap()
    build_perceiver(nc, *args, out)
    r = run_bass_kernel_spmd(nc, [arrays], core_ids=[0])
    return r.results[0]["out_x"]
```

```python
from contextlib import ExitStack

import concourse.bass as bass
from concourse import mybir

F32 = mybir.dt.float32
BF16 = mybir.dt.bfloat16
I32 = mybir.dt.int32
ALU = mybir.AluOpType
ACT = mybir.ActivationFunctionType
AX = mybir.AxisListType

P = 128
BANK = 512
HEAD_DIM = 32
LN_EPS = 1e-5
MASKED = -1e30
LOWEST = -3e38
TOP_K = 2


def build_perceiver(nc, x, ctx, mask, wq, bq, wk, bk, wv, bv, wf, bf, awq, awk, awv, awo,
                    ffn_w, ffn_b, router_w, router_b, out):
    _, S, D = x.shape
    KEYS = ctx.shape[1]
    E = ffn_w.shape[0]
    H = D // HEAD_DIM
    SCALE = float(HEAD_DIM) ** -0.5
    QT = S // P
    C = D // P
    HG = P // HEAD_DIM
    CHUNK = BANK
    KT = CHUNK // P
    NCHUNK = KEYS // CHUNK
    GROUP = 7
    NGROUP = NCHUNK // GROUP
    PIECE = GROUP * CHUNK
    ACT_CHUNKS = 3
    assert QT == 2 and C == 4 and NGROUP * GROUP == NCHUNK and NCHUNK * CHUNK == KEYS and E == 8

    weights = [wq, wk, wv, awq, awk, awv, wf, awo]
    WQ, WK, WV, AWQ, AWK, AWV, WF, AWO = range(8)
    SLOT = {WQ: 0, WF: 1, AWO: 0}
    PAIR = {WK: 0, WV: 1, AWQ: 2, AWK: 3, AWV: 4}
    NSTAGE = 3
    EARLY_SCANS = {AWQ: 0}
    NEARLY = len(EARLY_SCANS)
    SCAN_AFTER = (3, 8, 13)
    TURNED = 6

    mask_q = mask.rearrange("a b (t p) k -> p (a b t) k", p=P)
    ctx_k = ctx.rearrange("a k d -> (a k) d")

    with ExitStack() as es:
        def sb(name, shape, dt=F32):
            return es.enter_context(nc.sbuf_tensor(name, shape, dt))

        def sem(name):
            return es.enter_context(nc.semaphore(name))

        def pair(name, shape):
            return sb(name + "_high", shape, BF16), sb(name + "_low", shape, BF16)

        ident = sb("ident", [P, P])
        ones_row = sb("ones_row", [1, P])
        bit_weight = sb("bit_weight", [1, GROUP])
        window = sb("window", [P, 2 * P])
        lower = sb("lower", [P, E, E])
        stage = sb("stage", [P, NSTAGE, C, D])
        wT = sb("wT", [P, 2, C, D])
        wT_high, wT_low = pair("wT", [P, 5, C, D])
        scan = sb("scan", [P, QT, PIECE], I32)
        q2_pad = scan[:, :, :].bitcast(F32).rearrange("p t k -> p (t k)")[:, 0:H * S]\
            .rearrange("p (h q) -> p h q", h=H)
        pT_all = sb("pT_all", [P, TURNED * KT * S])
        pT = pT_all[:, :].rearrange("p (b k q) -> p b k q", b=TURNED, k=KT)
        pT2 = pT_all[:, 0:H * 3 * P].rearrange("p (h k) -> p h k", h=H)
        probs_all = sb("probs_all", [P, 3 * QT * CHUNK])
        probs = probs_all[:, :].rearrange("p (b t k) -> p b t k", b=3, t=QT)
        probs2 = probs_all[:, 0:3 * 3 * P].rearrange("p (b k) -> p b k", b=3)
        q_full = probs_all[:, 0:C * S].rearrange("p (g q) -> p g q", g=C)
        q_high = probs_all[:, 1024:1536].bitcast(BF16).rearrange("p (g q) -> p g q", g=C)
        q_low = probs_all[:, 1536:2048].bitcast(BF16).rearrange("p (g q) -> p g q", g=C)
        q_stack = sb("q_stack", [P, H, S], BF16)
        stage_flat = stage[:, :, :, :].rearrange("p b c d -> p (b c d)")
        k_stack = stage_flat[:, 0:H * CHUNK // 2].bitcast(BF16)\
            .rearrange("p (h k) -> p h k", h=H)
        ctx_in = stage_flat[:, H * CHUNK // 2:].rearrange("p (t d) -> p t d", t=KT)
        ctxT_high, ctxT_low = pair("ctxT", [P, C, CHUNK])
        kT_all = sb("kT_all", [P, 2, C * CHUNK // 2])
        kT_high = kT_all[:, 0, :].bitcast(BF16).rearrange("p (c k) -> p c k", c=C)
        kT_low = kT_all[:, 1, :].bitcast(BF16).rearrange("p (c k) -> p c k", c=C)
        k2T = kT_all[:, 0, :].rearrange("p (c k) -> p c k", c=C)
        v = sb("v", [P, KT, D])
        mask_in = sb("mask_in", [P, QT, CHUNK], I32)
        mask_add = sb("mask_add", [P, QT, CHUNK])
        oT = sb("oT", [P, C, S])
        res = sb("res", [P, QT, D])
        xn = mask_add
        xT = sb("xT", [P, C, S])
        xT_high = xT[:, 0:2, :].rearrange("p c s -> p (c s)").bitcast(BF16).rearrange("p (c s) -> p c s", c=C)
        xT_low = xT[:, 2:4, :].rearrange("p c s -> p (c s)").bitcast(BF16).rearrange("p (c s) -> p c s", c=C)
        ln_stats = sb("ln_stats", [P, QT, 6])
        ln_mv = sb("ln_mv", [P, QT, 2])
        ln_rstd = sb("ln_rstd", [P, QT, 1])
        bias_rows = sb("bias_rows", [3 * C, P])
        bias_cols = sb("bias_cols", [P, 3, C])
        bf_row = sb("bf_row", [1, D])
        rb_row = sb("rb_row", [1, E])
        ffn_b_sb = sb("ffn_b_sb", [E, D])
        rw_rows = sb("rw_rows", [E, D])
        rwT = sb("rwT", [P, C, E])
        open_size = sb("open_size", [P, QT, GROUP])
        is_open = sb("is_open", [P, QT, GROUP])
        open_count = sb("open_count", [P, QT, GROUP + 1])
        flag = sb("flag", [P, QT, GROUP])
        bits = sb("bits", [1, GROUP + 1])
        row_shut = sb("row_shut", [P, QT])
        shut_flag = sb("shut_flag", [P, QT])
        words = sb("words", [1, NGROUP], I32)
        shut_word = sb("shut_word", [1, 1], I32)
        table_use = sb("table_use", [1, 4])
        gate = sb("gate", [P, QT, H])
        m_run = sb("m_run", [P, QT, H])
        m_new = sb("m_new", [P, QT, H])
        m_neg = sb("m_neg", [P, QT, H])
        m_diff = sb("m_diff", [P, QT, H])
        alpha = sb("alpha", [P, QT, H])
        chunk_sum = sb("chunk_sum", [P, QT, H])
        row_sum = sb("row_sum", [P, QT, H])
        row_inv = sb("row_inv", [P, QT, H])
        logit = sb("logit", [P, QT, E])
        r_max = sb("r_max", [P, QT, 1])
        score = sb("score", [P, QT, E])
        r_sum = sb("r_sum", [P, QT, 1])
        r_inv = sb("r_inv", [P, QT, 1])
        above = v[:, 0, 0:QT * E * E].rearrange("p (t e f) -> p t e f", t=QT, e=E)
        tied = v[:, 1, 0:QT * E * E].rearrange("p (t e f) -> p t e f", t=QT, e=E)
        chosenT = v[0:E, 2, 0:QT * P].rearrange("e (t q) -> e t q", t=QT)
        rank = sb("rank", [P, QT, E])
        chosen = sb("chosen", [P, QT, E])
        ps = [es.enter_context(nc.psum_tensor(f"bank{i}", [P, BANK], F32)) for i in range(8)]

        x_loaded = sem("x_loaded")
        small_loaded = sem("small_loaded")
        stage_loaded = [sem(f"stage_loaded{i}") for i in range(NSTAGE)]
        scan_loaded = sem("scan_loaded")
        q_stacked = sem("q_stacked")
        k_stacked = sem("k_stacked")
        ctx_loaded = sem("ctx_loaded")
        mask_loaded = sem("mask_loaded")
        out_stored = sem("out_stored")
        pool_step = sem("pool_step")
        consts_ready = sem("consts_ready")
        dve_step = sem("dve_step")
        var_ready = sem("var_ready")
        std_ready = sem("std_ready")
        norm_ready = sem("norm_ready")
        tile_full = sem("tile_full")
        tile_act = sem("tile_act")
        tile_dve = sem("tile_dve")
        scan_act = sem("scan_act")
        scan_dve = sem("scan_dve")
        q_full_ready = sem("q_full_ready")
        q_high_ready = sem("q_high_ready")
        q_low_ready = sem("q_low_ready")
        size_used = sem("size_used")
        words_ready = sem("words_ready")
        shut_ready = sem("shut_ready")
        zeros_ready = sem("zeros_ready")
        ctx_turned = sem("ctx_turned")
        mask_used = sem("mask_used")
        ring_full = sem("ring_full")
        ring_act = sem("ring_act")
        ring_dve = sem("ring_dve")
        neg_ready = sem("neg_ready")
        probs_ready = sem("probs_ready")
        pT_full = sem("pT_full")
        pT_act = sem("pT_act")
        pT_dve = sem("pT_dve")
        pv_full = sem("pv_full")
        diff_ready = sem("diff_ready")
        alpha_ready = sem("alpha_ready")
        alphaT_full = sem("alphaT_full")
        fold_step = sem("fold_step")
        neg2_ready = sem("neg2_ready")
        probs2_ready = sem("probs2_ready")
        pT2_full = sem("pT2_full")
        pT2_taken = sem("pT2_taken")
        pv2_full = sem("pv2_full")
        inv_ready = sem("inv_ready")
        wideT_full = sem("wideT_full")
        oT_ready = sem("oT_ready")
        proj_full = sem("proj_full")
        logits_full = sem("logits_full")
        shift_ready = sem("shift_ready")
        exp_ready = sem("exp_ready")
        chosen_ready = sem("chosen_ready")
        chosenT_full = sem("chosenT_full")
        chosenT_ready = sem("chosenT_ready")
        bias_full = sem("bias_full")
        y_full = sem("y_full")
        y_taken = sem("y_taken")
        out_ready = sem("out_ready")

        setup_tiles = [("x", 0), ("x", 1), ("small", 0)]
        setup_tiles += [("w", (WQ, o)) for o in range(C)] + [("q", g) for g in range(C)]
        for w in range(1, 8):
            setup_tiles += [("w", (w, o)) for o in range(C)]

        def taker(n, kind, a):
            if kind in ("q", "small"):
                return "dve"
            if kind == "w" and a[0] in PAIR:
                return "both"
            return "dve" if n % 2 else "act"

        takers = [taker(n, kind, a) for n, (kind, a) in enumerate(setup_tiles)]
        NSETUP = len(setup_tiles)
        w_tile = {a: n for n, (kind, a) in enumerate(setup_tiles) if kind == "w"}
        q_tile = [n for n, (kind, _) in enumerate(setup_tiles) if kind == "q"]
        LATE = NSETUP
        takers += ["both"] * QT + ["act", "dve"] * (C + QT // 2) + ["dve"] * H + ["act", "dve"]
        NLATE = len(takers) - LATE

        def act_took(n):
            return takers[:n + 1].count("act") + takers[:n + 1].count("both")

        def dve_took(n):
            return takers[:n + 1].count("dve") + takers[:n + 1].count("both")

        def taken(n):
            return (tile_act, act_took(n)) if takers[n] == "act" else (tile_dve, dve_took(n))

        RING = 4
        NTILE = 3 * C + QT * H
        RING_ACT = 2 * C + C // 2
        RING_DVE = 2 * C + C // 2 + QT * H
        NFULL = NTILE - KT
        NSTACK = 4 * HG
        FOLD = 9

        def ring_taken(n, d):
            if n < 2 * C:
                return ring_dve, ONE + d * RING_DVE + n + 1
            if n < 3 * C:
                k = n - 2 * C
                if k % 2 == 0:
                    return ring_act, d * RING_ACT + 2 * C + k // 2 + 1
                return ring_dve, ONE + d * RING_DVE + 2 * C + k // 2 + 1
            return ring_dve, ONE + d * RING_DVE + 2 * C + C // 2 + n - 3 * C + 1

        ONE = 1
        NCONST = 4 + 1 + GROUP + 3

        def scan_one(eng, scan, scanned):
            with eng.If(eng.snap(scanned) != NGROUP):
                scan(eng.snap(scanned, min_val=NEARLY, max_val=NGROUP - 1))
                eng.reg_add(scanned, scanned, 1)

        def open_chunks(eng, body, scan=None):
            done = eng.alloc_register("chunks_done")
            scanned = eng.alloc_register("groups_scanned")
            needed = eng.alloc_register("round_needed")
            word = eng.alloc_register("chunk_word")
            first = eng.alloc_register("first_chunk")
            eng.reg_mov(done, 0)
            eng.reg_mov(scanned, NEARLY)
            eng.reg_mov(needed, 1)
            with eng.Fori(0, 2) as rest:
                with eng.If(eng.snap(needed) != 0):
                    eng.reg_mov(first, NCHUNK - GROUP)
                    with eng.Fori(0, NGROUP) as g:
                        if scan is not None:
                            with eng.If(eng.snap(scanned) == g):
                                scan(g)
                                eng.reg_add(scanned, scanned, 1)
                        eng.wait_ge(words_ready, g + 1)
                        eng.reg_mov(word, eng.value_load(words[0:1, bass.ds(g, 1)], min_val=0,
                                                         max_val=2 ** GROUP - 1))
                        eng.reg_alu(word, word, rest * (2 ** GROUP - 1), op=ALU.bitwise_xor)
                        with eng.If(eng.snap(word) != 0):
                            with eng.Fori(0, GROUP) as j:
                                with eng.If((eng.snap(word) & 1) != 0):
                                    body(eng.snap(first, min_val=0, max_val=NCHUNK - GROUP) + j,
                                         eng.snap(done, min_val=0, max_val=NCHUNK - 1), scanned)
                                    eng.reg_add(done, done, 1)
                                eng.reg_alu(word, word, 1, op=ALU.logical_shift_right)
                        eng.reg_sub(first, first, GROUP)
                eng.wait_ge(shut_ready, 1)
                eng.reg_mov(needed, eng.value_load(shut_word[0:1, 0:1], min_val=0, max_val=1))

        block = es.enter_context(nc.Block())

        @block.sync
        def _(sp):
            def load_weight(w):
                sp.dma_start(stage[:, w % NSTAGE, :, :], weights[w].rearrange("(o p) c -> p o c", p=P))\
                    .then_inc(stage_loaded[w % NSTAGE], 16)

            def load_expert(e):
                n = 8 + e
                sp.dma_start(stage[:, n % NSTAGE, :, :], ffn_w[e].rearrange("(c p) k -> p c k", p=P))\
                    .then_inc(stage_loaded[n % NSTAGE], 16)

            sp.dma_start(res[:, :, :], x.rearrange("a (t p) d -> p (a t) d", p=P)).then_inc(x_loaded, 16)
            for w in range(8):
                if w >= NSTAGE:
                    sp.wait_ge(tile_full, w_tile[(w - NSTAGE, C - 1)] + 1)
                load_weight(w)
            assert AWV % NSTAGE == 2
            sp.wait_ge(tile_full, w_tile[(AWV, C - 1)] + 1)

            def load_chunk(c, d, scanned):
                first = sp.snap(c * CHUNK)
                sp.wait_ge(mask_used, ONE + d)
                sp.wait_ge(ctx_turned, ONE + d * KT)
                sp.dma_start(mask_in[:, :, :], mask_q[:, :, bass.ds(first, CHUNK)])\
                    .then_inc(mask_loaded, 16)
                sp.dma_start(ctx_in, ctx_k[bass.ds(first, CHUNK), :]
                             .rearrange("(t p) d -> p t d", p=P)).then_inc(ctx_loaded, 16)
                stacked = k_stack.rearrange("p (g j) k -> p g j k", j=HG)
                for part, kT_part in enumerate((kT_high, kT_low)):
                    if part == 0:
                        sp.wait_ge(ring_full, ONE + d * NFULL)
                        sp.wait_ge(ring_act, d * RING_ACT + 2 * C)
                    else:
                        sp.wait_ge(ring_dve, ONE + d * RING_DVE + 2 * C)
                    for j in range(HG):
                        for slot in (2 * part, 2 * part + 1):
                            sp.dma_start(stacked[slot * HEAD_DIM:(slot + 1) * HEAD_DIM, :, j, :],
                                         kT_part[j * HEAD_DIM:(j + 1) * HEAD_DIM, :, :]).then_inc(k_stacked, 16)

            open_chunks(sp, load_chunk)
            sp.wait_ge(wideT_full, 1)
            for e in range(E):
                if e >= NSTAGE:
                    sp.wait_ge(y_full, QT * (e - NSTAGE + 1))
                load_expert(e)
            out_q = out.rearrange("a (t p) d -> p (a t) d", p=P)
            for t in range(QT):
                sp.wait_ge(out_ready, t + 1)
                sp.dma_start(out_q[:, t, :], res[:, t, :]).then_inc(out_stored, 16)
            sp.wait_ge(out_stored, 16 * QT)

        @block.gpsimd
        def _(pool):
            def load_group(g):
                first = (NGROUP - 1 - g) * PIECE
                for t in range(QT):
                    pool.dma_start(scan[:, t, :], mask_q[:, t, first:first + PIECE]).then_inc(scan_loaded, 16)

            pool.sem_inc(size_used, ONE)
            nc.gpsimd.memset(ident[:, :], 0.0).then_inc(pool_step, 1)
            nc.gpsimd.memset(window[:, :], 0.0).then_inc(pool_step, 1)
            nc.gpsimd.memset(lower[:, :, :], 1.0).then_inc(pool_step, 1)
            nc.gpsimd.memset(bits[:, :], 0.0).then_inc(pool_step, 1)
            nc.gpsimd.memset(open_count[:, :, :], 0.0).then_inc(pool_step, 1)
            pool.wait_ge(pool_step, 5)
            nc.gpsimd.affine_select(out=ident[:, :], in_=ident[:, :], compare_op=ALU.not_equal, fill=1.0,
                                    base=0, pattern=[[-1, P]], channel_multiplier=1).then_inc(consts_ready, 1)
            pool.wait_ge(stage_loaded[WK], 16)
            load_group(0)
            nc.gpsimd.affine_select(out=window[:, 0:P], in_=window[:, 0:P], compare_op=ALU.is_ge, fill=MASKED,
                                    base=-1, pattern=[[1, P]], channel_multiplier=-1).then_inc(consts_ready, 1)
            nc.gpsimd.affine_select(out=window[:, P:], in_=window[:, P:], compare_op=ALU.is_ge, fill=MASKED,
                                    base=0, pattern=[[-1, P]], channel_multiplier=1).then_inc(consts_ready, 1)
            nc.gpsimd.affine_select(out=lower[:, :, :], in_=lower[:, :, :], compare_op=ALU.is_ge, fill=0.0,
                                    base=-1, pattern=[[1, E], [-1, E]], channel_multiplier=0)\
                .then_inc(consts_ready, 1)
            nc.gpsimd.memset(ones_row[:, :], 1.0).then_inc(consts_ready, 1)
            for j in range(GROUP):
                nc.gpsimd.memset(bit_weight[:, j:j + 1], float(2 ** j)).then_inc(consts_ready, 1)
            nc.gpsimd.memset(oT[:, :, :], 0.0).then_inc(consts_ready, 1)
            nc.gpsimd.memset(m_run[:, :, :], LOWEST).then_inc(consts_ready, 1)
            nc.gpsimd.memset(row_sum[:, :, :], 0.0).then_inc(consts_ready, 1)
            pool.wait_ge(consts_ready, NCONST)

            steps = [5]

            def link(ins):
                steps[0] += 1
                ins.then_inc(pool_step, 1)
                pool.wait_ge(pool_step, steps[0])

            for g in range(NGROUP):
                pool.wait_ge(scan_act, g + 1)
                pool.wait_ge(scan_dve, g + 1)
                link(nc.gpsimd.tensor_scalar(is_open[:, :, :], open_size[:, :, :], 0.0, None, ALU.is_gt))
                pool.sem_inc(size_used, 1)
                if g == 0:
                    pool.wait_ge(stage_loaded[AWO % NSTAGE], 16 * (AWO // NSTAGE + 1))
                if g + 1 < NGROUP:
                    load_group(g + 1)
                link(nc.gpsimd.tensor_tensor(open_count[:, :, 0:GROUP], open_count[:, :, 0:GROUP], is_open[:, :, :],
                                             ALU.add))
                link(nc.gpsimd.partition_all_reduce(flag[:, :, :].rearrange("p t j -> p (t j)"),
                                                    is_open[:, :, :].rearrange("p t j -> p (t j)"), P,
                                                    bass.bass_isa.ReduceOp.max))
                link(nc.gpsimd.tensor_tensor(bits[:, 0:GROUP], flag[0:1, 0, :], flag[0:1, 1, :], ALU.add))
                link(nc.gpsimd.tensor_scalar(bits[:, 0:GROUP], bits[:, 0:GROUP], 0.0, None, ALU.is_gt))
                link(nc.gpsimd.tensor_tensor(bits[:, 0:GROUP], bits[:, 0:GROUP], bit_weight[:, :], ALU.mult))
                for half in (4, 2, 1):
                    link(nc.gpsimd.tensor_tensor(bits[:, 0:half], bits[:, 0:half], bits[:, half:2 * half], ALU.add))
                nc.gpsimd.tensor_copy(words[:, g:g + 1], bits[:, 0:1]).then_inc(words_ready, 1)
            for half in (4, 2, 1):
                link(nc.gpsimd.tensor_tensor(open_count[:, :, 0:half], open_count[:, :, 0:half],
                                             open_count[:, :, half:2 * half], ALU.add))
            link(nc.gpsimd.tensor_scalar(row_shut[:, :], open_count[:, :, 0], 0.0, None, ALU.is_equal))
            link(nc.gpsimd.partition_all_reduce(shut_flag[:, :], row_shut[:, :], P, bass.bass_isa.ReduceOp.max))
            link(nc.gpsimd.tensor_tensor(bits[:, 0:1], shut_flag[0:1, 0:1], shut_flag[0:1, 1:2], ALU.add))
            link(nc.gpsimd.tensor_scalar(bits[:, 0:1], bits[:, 0:1], 0.0, None, ALU.is_gt))
            nc.gpsimd.tensor_copy(shut_word[:, :], bits[:, 0:1]).then_inc(shut_ready, 1)
            nc.gpsimd.memset(q2_pad, 0.0).then_inc(zeros_ready, 1)

        @block.tensor
        def _(pe):
            def spread(a):
                for g in range(C):
                    for t in range(QT):
                        at = (g % 2) * S + t * P
                        for j in range(HG):
                            rows = slice(j * HEAD_DIM, (j + 1) * HEAD_DIM)
                            h = HG * g + j
                            last = nc.tensor.matmul(ps[4 + g // 2][rows, at:at + P],
                                                    a[:, t, h:h + 1].broadcast_to([P, HEAD_DIM]), ident[:, :],
                                                    start=True, stop=True, tile_position=(0, j * HEAD_DIM))
                return last

            def transpose(o, i, n=P):
                return nc.tensor.transpose(o, i, ident[0:n, 0:n])

            def setup_tile(n):
                kind, a = setup_tiles[n]
                if n >= 8:
                    pe.wait_ge(*taken(n - 8))
                b = ps[n % 8]
                if kind == "x":
                    pe.wait_ge(norm_ready, a + 1)
                    for c in range(C):
                        last = transpose(b[:, c * P:(c + 1) * P], xn[:, a, c * P:(c + 1) * P])
                elif kind == "small":
                    pe.wait_ge(small_loaded, 16 * 7)
                    transpose(b[:, 0:3 * C], bias_rows[:, :], 3 * C)
                    for c in range(C):
                        last = transpose(b[:, 64 + c * E:64 + (c + 1) * E], rw_rows[:, c * P:(c + 1) * P], E)
                elif kind == "w":
                    w, o = a
                    pe.wait_ge(stage_loaded[w % NSTAGE], 16 * (w // NSTAGE + 1))
                    for c in range(C):
                        last = transpose(b[:, c * P:(c + 1) * P], stage[:, w % NSTAGE, o, c * P:(c + 1) * P])
                else:
                    if a == 0:
                        pe.wait_ge(*taken(0))
                        pe.wait_ge(*taken(1))
                        pe.wait_ge(*taken(w_tile[(WQ, C - 2)]))
                        pe.wait_ge(*taken(w_tile[(WQ, C - 1)]))
                    for c in range(C):
                        last = nc.tensor.matmul(b[:, 0:S], wT[:, SLOT[WQ], c, a * P:(a + 1) * P], xT[:, c, :],
                                                start=(c == 0), stop=(c == C - 1))
                last.then_inc(tile_full, 1)

            pe.sem_inc(ctx_turned, ONE)
            pe.sem_inc(pT_full, ONE)
            pe.sem_inc(ring_full, ONE)
            pe.wait_ge(consts_ready, NCONST)
            for n in range(NSETUP):
                setup_tile(n)
            pe.wait_ge(tile_act, act_took(NSETUP - 1))
            pe.wait_ge(tile_dve, dve_took(NSETUP - 1))
            pe.wait_ge(q_stacked, 16 * NSTACK)

            def products(b, stationary, moving):
                terms = [(c, i, j) for c in range(C) for i, j in ((0, 0), (0, 1), (1, 0))]
                for n, (c, i, j) in enumerate(terms):
                    last = nc.tensor.matmul(b, stationary(i, c), moving(j, c), start=(n == 0),
                                            stop=(n == len(terms) - 1))
                return last

            wT_parts = (wT_high, wT_low)
            ctxT_parts = (ctxT_high, ctxT_low)
            xT_parts = (xT_high, xT_low)

            def chunk(c, d, scanned):
                def ring(n, waits=()):
                    if n < RING:
                        pe.wait_ge(ring_dve, ONE + d * RING_DVE)
                    else:
                        pe.wait_ge(*ring_taken(n - RING, d))
                    for s, value in waits:
                        pe.wait_ge(s, value)
                    return ps[n % RING]

                for k in range(KT):
                    b = ring(k, [(ctx_loaded, d * 16 + 16)])
                    for cc in range(C):
                        last = transpose(b[:, cc * P:(cc + 1) * P], ctx_in[:, k, cc * P:(cc + 1) * P])
                    last.then_inc(ctx_turned, 1)
                for g in range(C):
                    b = ring(C + g, [ring_taken(3, d)])
                    products(b[:, :], lambda i, cc: wT_parts[i][:, PAIR[WK], cc, g * P:(g + 1) * P],
                             lambda i, cc: ctxT_parts[i][:, cc, :]).then_inc(ring_full, 1)
                for k in range(KT):
                    b = ring(2 * C + k)
                    products(b[:, :], lambda i, cc: ctxT_parts[i][:, cc, k * P:(k + 1) * P],
                             lambda i, cc: wT_parts[i][:, PAIR[WV], cc, :]).then_inc(ring_full, 1)

                def scores(h):
                    for t in range(QT):
                        b = ps[t]
                        pe.wait_ge(*ring_taken(3 * C + QT * (h - 1) + t if h else 2 * C + t, d))
                        if h == 0 and t == 0:
                            pe.wait_ge(k_stacked, (d + 1) * 16 * NSTACK)
                        nc.tensor.matmul(b[:, :], q_stack[:, h, t * P:(t + 1) * P], k_stack[:, h, :],
                                         start=True, stop=True).then_inc(ring_full, 1)

                def turn_probs(h):
                    for t in range(QT):
                        m = QT * h + t
                        pe.wait_ge(probs_ready, d * QT * H + m + 1)
                        if h >= 2:
                            pe.wait_ge(pT_act if t == 0 else pT_dve, d * H + h - 1)
                        elif h == 0:
                            pe.wait_ge(*ring_taken(2 * C + 2 + t, d))
                        elif t == 0:
                            pe.wait_ge(fold_step, ONE + d * FOLD)
                        b = ps[2 + m % 4]
                        for k in range(KT):
                            last = transpose(b[:, k * P:(k + 1) * P], probs[:, h % 3, t, k * P:(k + 1) * P])
                        last.then_inc(pT_full, 1)

                def weigh_values(g):
                    pe.wait_ge(pT_act, d * H + HG * (g + 1))
                    pe.wait_ge(pT_dve, d * H + HG * (g + 1))
                    if g == 0:
                        pe.wait_ge(*ring_taken(3 * C - 2, d))
                        pe.wait_ge(*ring_taken(3 * C - 1, d))
                    b = ps[6 + g // 2]
                    for k in range(KT):
                        for j in range(HG):
                            h = HG * g + j
                            rows = slice(j * HEAD_DIM, (j + 1) * HEAD_DIM)
                            last = nc.tensor.matmul(b[rows, (g % 2) * S:(g % 2 + 1) * S],
                                                    v[:, k, h * HEAD_DIM:(h + 1) * HEAD_DIM],
                                                    pT[:, h % TURNED, k, :], start=(k == 0), stop=(k == KT - 1),
                                                    tile_position=(0, j * HEAD_DIM))
                    last.then_inc(pv_full, 1)

                for i in range(H + 3):
                    if i < H:
                        scores(i)
                    if 2 <= i < H + 2:
                        turn_probs(i - 2)
                    if i >= 6 and (i - 6) % HG == 0:
                        weigh_values((i - 6) // HG)
                pe.wait_ge(alpha_ready, d + 1)
                spread(alpha).then_inc(alphaT_full, 1)

            open_chunks(pe, chunk)

            def project(w, n, bias_row=None):
                if bias_row is not None:
                    for t in range(QT):
                        nc.tensor.matmul(ps[t][:, :], ones_row[:, :], bias_row[:, :], start=True, stop=False)
                pe.wait_ge(oT_ready, n)
                for t in range(QT):
                    for g in range(C):
                        last = nc.tensor.matmul(ps[t][:, :], oT[:, g, t * P:(t + 1) * P], wT[:, SLOT[w], g, :],
                                                start=(g == 0 and bias_row is None), stop=(g == C - 1))
                    last.then_inc(proj_full, 1)

            pe.wait_ge(inv_ready, 1)
            spread(row_inv).then_inc(wideT_full, 1)
            project(WF, 1, bf_row)

            def late(n):
                if n >= RING:
                    pe.wait_ge(*taken(LATE + n - RING))
                return ps[n % RING]

            def late_wait(n):
                pe.wait_ge(*taken(LATE + n))

            for t in range(QT):
                b = late(t)
                pe.wait_ge(norm_ready, QT + t + 1)
                for c in range(C):
                    last = transpose(b[:, c * P:(c + 1) * P], xn[:, t, c * P:(c + 1) * P])
                last.then_inc(tile_full, 1)
            late_wait(0)
            late_wait(1)
            for i, w in enumerate((AWQ, AWK)):
                for g in range(C):
                    b = late(QT + C * i + g)
                    products(b[:, 0:S], lambda i, c: wT_parts[i][:, PAIR[w], c, g * P:(g + 1) * P],
                             lambda i, c: xT_parts[i][:, c, :]).then_inc(tile_full, 1)
            for t in range(QT):
                b = late(QT + 2 * C + t)
                products(b[:, :], lambda i, c: xT_parts[i][:, c, t * P:(t + 1) * P],
                         lambda i, c: wT_parts[i][:, PAIR[AWV], c, :]).then_inc(tile_full, 1)

            def scores2(h):
                b = late(2 * QT + 2 * C + h)
                if h % HG == 0:
                    late_wait(QT + h // HG)
                    late_wait(QT + C + h // HG)
                k2 = k2T[:, h // HG, :]
                nc.tensor.matmul(b[:, 0:P], q2_pad[:, h, 0:P], k2[:, 0:P], start=True, stop=True)
                nc.tensor.matmul(b[:, P:3 * P], q2_pad[:, h, P:2 * P], k2[:, :], start=True, stop=True)\
                    .then_inc(tile_full, 1)

            def turn_probs2(h):
                pe.wait_ge(probs2_ready, h + 1)
                if h >= 2:
                    pe.wait_ge(pT2_taken, h - 1)
                b = ps[4 + h % 2]
                for k in range(3):
                    last = transpose(b[:, k * P:(k + 1) * P], probs2[:, h % 3, k * P:(k + 1) * P])
                last.then_inc(pT2_full, 1)

            def weigh_values2(g):
                pe.wait_ge(pT2_taken, HG * (g + 1))
                if g == 0:
                    late_wait(QT + 2 * C)
                    late_wait(QT + 2 * C + 1)
                b = ps[6 + g // 2]
                at = (g % 2) * S
                for k, vt, col, first, final in ((0, 0, 0, True, True), (1, 0, P, True, False),
                                                 (2, 1, P, False, True)):
                    for j in range(HG):
                        h = HG * g + j
                        rows = slice(j * HEAD_DIM, (j + 1) * HEAD_DIM)
                        last = nc.tensor.matmul(b[rows, at + col:at + col + P],
                                                v[:, vt, h * HEAD_DIM:(h + 1) * HEAD_DIM],
                                                pT2[:, h, k * P:(k + 1) * P], start=first, stop=final,
                                                tile_position=(0, j * HEAD_DIM))
                last.then_inc(pv2_full, 1)

            for i in range(H + 3):
                if i < H:
                    scores2(i)
                if 2 <= i < H + 2:
                    turn_probs2(i - 2)
                if i >= 6 and (i - 6) % HG == 0:
                    weigh_values2((i - 6) // HG)
            pe.wait_ge(inv_ready, 2)
            spread(row_inv).then_inc(wideT_full, 1)
            project(AWO, 2)

            for t in range(QT):
                pe.wait_ge(norm_ready, 2 * QT + t + 1)
                for c in range(C):
                    last = transpose(ps[2 + t][:, c * P:(c + 1) * P], xn[:, t, c * P:(c + 1) * P])
                last.then_inc(tile_full, 1)
            pe.wait_ge(*taken(LATE + NLATE - 2))
            pe.wait_ge(*taken(LATE + NLATE - 1))
            for t in range(QT):
                nc.tensor.matmul(ps[4][:, t * E:(t + 1) * E], ones_row[:, :], rb_row[:, :], start=True, stop=False)
                for c in range(C):
                    last = nc.tensor.matmul(ps[4][:, t * E:(t + 1) * E], xT[:, c, t * P:(t + 1) * P],
                                            rwT[:, c, :], start=False, stop=(c == C - 1))
            last.then_inc(logits_full, 1)

            def expert(n):
                e, t = n // QT, n % QT
                pe.wait_ge(stage_loaded[(8 + e) % NSTAGE], 16 * ((8 + e) // NSTAGE + 1))
                if n >= 4:
                    pe.wait_ge(y_taken, n - 3)
                b = ps[n % 4]
                for c in range(C):
                    last = nc.tensor.matmul(b[:, :], xT[:, c, t * P:(t + 1) * P], stage[:, (8 + e) % NSTAGE, c, :],
                                            start=(c == 0), stop=(c == C - 1))
                last.then_inc(y_full, 1)

            for n in range(4):
                expert(n)
            pe.wait_ge(chosen_ready, 1)
            for t in range(QT):
                last = transpose(ps[5][0:E, t * P:(t + 1) * P], chosen[:, t, :])
            last.then_inc(chosenT_full, 1)
            pe.wait_ge(chosenT_ready, 1)
            for t in range(QT):
                last = nc.tensor.matmul(ps[6 + t][:, :], chosenT[:, t, :], ffn_b_sb[:, :], start=True, stop=True)
            last.then_inc(bias_full, 1)
            for n in range(4, QT * E):
                expert(n)


        @block.scalar
        def _(act):
            for i, b in enumerate((bq, bk, bv)):
                act.dma_start(bias_rows[C * i:C * (i + 1), :], b.rearrange("(c p) -> c p", p=P))\
                    .then_inc(small_loaded, 16)
            act.dma_start(rw_rows[:, :], router_w).then_inc(small_loaded, 16)
            act.dma_start(bf_row[:, :], bf.rearrange("(a d) -> a d", a=1)).then_inc(small_loaded, 16)
            act.dma_start(rb_row[:, :], router_b.rearrange("(a d) -> a d", a=1)).then_inc(small_loaded, 16)
            act.dma_start(ffn_b_sb[:, :], ffn_b).then_inc(small_loaded, 16)

            def layer_norm_root(n):
                act.wait_ge(var_ready, n)
                nc.scalar.activation(ln_rstd[:, :, :], ln_rstd[:, :, :], ACT.Sqrt).then_inc(std_ready, 1)
                if n > 1:
                    load_table(ACT.Exp)

            def load_table(function):
                nc.scalar.activation(table_use[:, loads[0]:loads[0] + 1], ones_row[:, 0:1], function)
                loads[0] += 1

            loads = [0]
            layer_norm_root(1)

            def take_setup(n):
                kind, a = setup_tiles[n]
                act.wait_ge(tile_full, n + 1)
                if kind == "x":
                    dst = xT[:, :, a * P:(a + 1) * P]
                else:
                    w, o = a
                    if w == AWO and o < 2:
                        act.wait_ge(tile_full, q_tile[-1] + 1)
                    dst = wT_high[:, PAIR[w], :, o * P:(o + 1) * P] if w in PAIR else \
                        wT[:, SLOT[w], :, o * P:(o + 1) * P]
                nc.scalar.activation(dst, ps[n % 8][:, :].rearrange("p (c q) -> p c q", c=C), ACT.Copy)\
                    .then_inc(tile_act, 1)

            def scan_group(g):
                act.wait_ge(size_used, ONE + g)
                act.wait_ge(scan_loaded, (g + 1) * 16 * QT)
                for t in range(QT):
                    for i in range(GROUP - ACT_CHUNKS, GROUP):
                        piece = scan[:, t, i * CHUNK:(i + 1) * CHUNK]
                        last = nc.scalar.activation(piece.bitcast(F32), piece, ACT.Abs,
                                                    accum_out=open_size[:, t, i:i + 1])
                last.then_inc(scan_act, 1)

            for n in range(w_tile[(0, 0)]):
                if takers[n] == "act":
                    take_setup(n)
            for w in range(8):
                for o in range(C):
                    if takers[w_tile[(w, o)]] != "dve":
                        take_setup(w_tile[(w, o)])
                if w == WQ:
                    act.wait_ge(q_full_ready, 1)
                    nc.scalar.activation(q_high, q_full, ACT.Copy).then_inc(q_high_ready, 1)
                if w in EARLY_SCANS:
                    scan_group(EARLY_SCANS[w])
                if w == WV:
                    stacked = q_stack[:, :, :].rearrange("p (g j) q -> p g j q", j=HG)
                    act.wait_ge(q_high_ready, 1)
                    act.wait_ge(q_low_ready, 1)
                    for j in range(HG):
                        for slot in range(4):
                            act.dma_start(stacked[slot * HEAD_DIM:(slot + 1) * HEAD_DIM, :, j, :],
                                          (q_high, q_low)[slot % 2][j * HEAD_DIM:(j + 1) * HEAD_DIM, :, :])\
                                .then_inc(q_stacked, 16)

            def chunk(c, d, scanned):
                for n in range(KT):
                    act.wait_ge(ctx_turned, ONE + d * KT + n + 1)
                    nc.scalar.activation(ctxT_high[:, :, n * P:(n + 1) * P],
                                         ps[n % RING][:, :].rearrange("p (c k) -> p c k", c=C), ACT.Copy)\
                        .then_inc(ring_act, 1)
                for g in range(C):
                    act.wait_ge(ring_full, ONE + d * NFULL + g + 1)
                    nc.scalar.activation(kT_high[:, g, :], ps[(C + g) % RING][:, :], ACT.Identity,
                                         bias=bias_cols[:, 1, g:g + 1]).then_inc(ring_act, 1)
                for k in (0, 2):
                    act.wait_ge(ring_full, ONE + d * NFULL + C + k + 1)
                    nc.scalar.activation(v[:, k, :], ps[(2 * C + k) % RING][:, :], ACT.Copy).then_inc(ring_act, 1)
                for i in range(H + 2):
                    if i < H:
                        act.wait_ge(neg_ready, d * H + i + 1)
                        for t in range(QT):
                            nc.scalar.activation(probs[:, i % 3, t, :], probs[:, i % 3, t, :], ACT.Exp,
                                                 bias=m_neg[:, t, i:i + 1],
                                                 accum_out=chunk_sum[:, t, i:i + 1]).then_inc(probs_ready, 1)
                    if i == H:
                        act.wait_ge(diff_ready, d + 1)
                        nc.scalar.activation(alpha[:, :, :], m_diff[:, :, :], ACT.Exp).then_inc(alpha_ready, 1)
                    if i >= 2:
                        h = i - 2
                        act.wait_ge(pT_full, ONE + d * QT * H + QT * h + 1)
                        if h >= TURNED:
                            act.wait_ge(pv_full, d * C + (h - TURNED) // HG + 1)
                        nc.scalar.activation(pT[:, h % TURNED, :, 0:P],
                                             ps[2 + QT * h % 4][:, :].rearrange("p (k q) -> p k q", k=KT),
                                             ACT.Copy).then_inc(pT_act, 1)
                    if i in SCAN_AFTER:
                        scan_one(act, scan_group, scanned)

            open_chunks(act, chunk, scan_group)

            load_table(ACT.Sqrt)
            layer_norm_root(2)
            for t in range(QT):
                act.wait_ge(tile_full, LATE + t + 1)
                nc.scalar.activation(xT_high[:, :, t * P:(t + 1) * P],
                                     ps[t][:, :].rearrange("p (c q) -> p c q", c=C), ACT.Copy).then_inc(tile_act, 1)
            act.wait_ge(zeros_ready, 1)
            for g in (0, 2):
                n = QT + g
                act.wait_ge(tile_full, LATE + n + 1)
                for j in range(HG):
                    rows = slice(j * HEAD_DIM, (j + 1) * HEAD_DIM)
                    last = nc.scalar.activation(q2_pad[rows, HG * g + j, :], ps[n % RING][rows, 0:S], ACT.Copy,
                                                scale=SCALE)
                last.then_inc(tile_act, 1)
            for g in (0, 2):
                n = QT + C + g
                act.wait_ge(tile_full, LATE + n + 1)
                nc.scalar.activation(k2T[:, g, :], ps[n % RING][:, 0:S], ACT.Copy).then_inc(tile_act, 1)
            n = QT + 2 * C
            act.wait_ge(tile_full, LATE + n + 1)
            nc.scalar.activation(v[:, 0, :], ps[n % RING][:, :], ACT.Copy).then_inc(tile_act, 1)
            for h in range(H):
                act.wait_ge(neg2_ready, h + 1)
                nc.scalar.activation(probs2[:, h % 3, 0:P], probs2[:, h % 3, 0:P], ACT.Exp,
                                     bias=m_neg[:, 0, h:h + 1], accum_out=row_sum[:, 0, h:h + 1])
                nc.scalar.activation(probs2[:, h % 3, P:], probs2[:, h % 3, P:], ACT.Exp,
                                     bias=m_neg[:, 1, h:h + 1], accum_out=row_sum[:, 1, h:h + 1])\
                    .then_inc(probs2_ready, 1)

            load_table(ACT.Sqrt)
            layer_norm_root(3)
            act.wait_ge(tile_full, LATE + NLATE - 1)
            nc.scalar.activation(xT[:, :, 0:P], ps[2][:, :].rearrange("p (c q) -> p c q", c=C), ACT.Copy)\
                .then_inc(tile_act, 1)
            act.wait_ge(shift_ready, 1)
            nc.scalar.activation(score[:, :, :], logit[:, :, :], ACT.Exp).then_inc(exp_ready, 1)
            act.wait_ge(chosenT_full, 1)
            nc.scalar.activation(chosenT[:, :, :], ps[5][0:E, 0:QT * P].rearrange("e (t q) -> e t q", t=QT), ACT.Copy)\
                .then_inc(chosenT_ready, 1)

        @block.vector
        def _(dve):
            steps = [0]
            norms = [0]

            def link(ins):
                steps[0] += 1
                ins.then_inc(dve_step, 1)
                dve.wait_ge(dve_step, steps[0])

            def layer_norm():
                for t in range(QT):
                    last = nc.vector.bn_stats(ln_stats[:, t, :], res[:, t, :])
                link(last)
                for t in range(QT):
                    last = nc.vector.bn_aggr(ln_mv[:, t, :], ln_stats[:, t, :])
                link(last)
                nc.vector.tensor_scalar(ln_rstd[:, :, :], ln_mv[:, :, 1:2], LN_EPS, None, ALU.add)\
                    .then_inc(var_ready, 1)
                norms[0] += 1
                dve.wait_ge(std_ready, norms[0])
                link(nc.vector.reciprocal(ln_rstd[:, :, :], ln_rstd[:, :, :]))
                for t in range(QT):
                    nc.vector.tensor_scalar(xn[:, t, :], res[:, t, :], ln_mv[:, t, 0:1], ln_rstd[:, t, :],
                                            ALU.subtract, ALU.mult).then_inc(norm_ready, 1)

            def take_setup(n):
                kind, a = setup_tiles[n]
                dve.wait_ge(tile_full, n + 1)
                b = ps[n % 8]
                quarters = b[:, :].rearrange("p (c q) -> p c q", c=C)
                if kind == "x":
                    last = nc.vector.tensor_copy(xT[:, :, a * P:(a + 1) * P], quarters)
                elif kind == "w":
                    w, o = a
                    if w in PAIR:
                        dve.wait_ge(tile_act, act_took(n))
                        last = nc.vector.tensor_tensor(wT_low[:, PAIR[w], :, o * P:(o + 1) * P], quarters,
                                                       wT_high[:, PAIR[w], :, o * P:(o + 1) * P], ALU.subtract)
                    else:
                        last = nc.vector.tensor_copy(wT[:, SLOT[w], :, o * P:(o + 1) * P], quarters)
                elif kind == "small":
                    link(nc.vector.tensor_copy(bias_cols[:, :, :], b[:, 0:3 * C].rearrange("p (i c) -> p i c", i=3)))
                    last = nc.vector.tensor_copy(rwT[:, :, :], b[:, 64:64 + C * E].rearrange("p (c e) -> p c e", c=C))
                else:
                    last = nc.vector.tensor_scalar(q_full[:, a, :], b[:, 0:S], bias_cols[:, 0, a:a + 1], SCALE,
                                                   ALU.add, ALU.mult)
                last.then_inc(tile_dve, 1)

            def scan_group(g):
                n = GROUP - ACT_CHUNKS
                dve.wait_ge(size_used, ONE + g)
                dve.wait_ge(scan_loaded, (g + 1) * 16 * QT)
                for t in range(QT):
                    last = nc.vector.tensor_reduce(open_size[:, t, 0:n],
                                                   scan[:, t, 0:n * CHUNK].rearrange("p (c k) -> p c k", c=n),
                                                   AX.X, ALU.max, apply_absolute_value=True)
                last.then_inc(scan_dve, 1)

            for starts_at_one in (mask_used, ring_dve, fold_step):
                dve.sem_inc(starts_at_one, ONE)
            dve.wait_ge(x_loaded, 16)
            layer_norm()
            for n in range(3):
                if takers[n] == "dve":
                    take_setup(n)
            for w in range(8):
                for o in range(C):
                    if takers[w_tile[(w, o)]] != "act":
                        take_setup(w_tile[(w, o)])
                if w == WQ:
                    for n in q_tile:
                        take_setup(n)
                    dve.wait_ge(*taken(q_tile[-1]))
                    dve.sem_inc(q_full_ready, 1)
                    dve.wait_ge(q_high_ready, 1)
                    nc.vector.tensor_tensor(q_low, q_full, q_high, ALU.subtract).then_inc(q_low_ready, 1)
                if w in EARLY_SCANS:
                    scan_group(EARLY_SCANS[w])

            def chunk(c, d, scanned):
                dve.wait_ge(mask_loaded, d * 16 + 16)
                fold = [0]

                def fold_link(ins):
                    fold[0] += 1
                    ins.then_inc(fold_step, 1)
                    dve.wait_ge(fold_step, ONE + d * FOLD + fold[0])

                fold_link(nc.vector.tensor_scalar(mask_add[:, :, :], mask_in[:, :, :], 0.0, MASKED,
                                                  ALU.is_equal, ALU.mult))
                dve.sem_inc(mask_used, 1)
                for n in range(KT):
                    dve.wait_ge(ring_act, d * RING_ACT + n + 1)
                    nc.vector.tensor_tensor(ctxT_low[:, :, n * P:(n + 1) * P],
                                            ps[n % RING][:, :].rearrange("p (c k) -> p c k", c=C),
                                            ctxT_high[:, :, n * P:(n + 1) * P], ALU.subtract).then_inc(ring_dve, 1)
                for g in range(C):
                    dve.wait_ge(ring_act, d * RING_ACT + C + g + 1)
                    nc.vector.scalar_tensor_tensor(out=kT_low[:, g, :], in0=ps[(C + g) % RING][:, :],
                                                   scalar=bias_cols[:, 1, g:g + 1], in1=kT_high[:, g, :],
                                                   op0=ALU.add, op1=ALU.subtract).then_inc(ring_dve, 1)
                for k in (1, 3):
                    dve.wait_ge(ring_full, ONE + d * NFULL + C + k + 1)
                    nc.vector.tensor_copy(v[:, k, :], ps[(2 * C + k) % RING][:, :]).then_inc(ring_dve, 1)
                for i in range(H + 2):
                    if i < H:
                        if i >= 3:
                            dve.wait_ge(pT_full, ONE + d * QT * H + QT * (i - 2))
                        else:
                            dve.wait_ge(pT_full, ONE + d * QT * H)
                        for t in range(QT):
                            n = 3 * C + QT * i + t
                            dve.wait_ge(ring_full, ONE + d * NFULL + n - KT + 1)
                            nc.vector.memset(gate[:, t, i:i + 1], 0.0)
                            nc.vector.tensor_tensor_reduce(probs[:, i % 3, t, :], ps[t][:, :], mask_add[:, t, :],
                                                           1.0, m_run[:, t, i:i + 1], ALU.add, ALU.max,
                                                           m_new[:, t, i:i + 1]).then_inc(ring_dve, 1)
                        dve.wait_ge(ring_dve, ONE + d * RING_DVE + 2 * C + C // 2 + QT * (i + 1))
                        nc.vector.tensor_scalar(m_neg[:, :, i:i + 1], m_new[:, :, i:i + 1], -1.0, None, ALU.mult)\
                            .then_inc(neg_ready, 1)
                    if i == H - 1:
                        fold_link(nc.vector.tensor_tensor(m_diff[:, :, :], m_run[:, :, :], m_new[:, :, :],
                                                          ALU.subtract))
                        dve.sem_inc(diff_ready, 1)
                    if i >= 2:
                        h = i - 2
                        dve.wait_ge(pT_full, ONE + d * QT * H + QT * h + 2)
                        if h >= TURNED:
                            dve.wait_ge(pv_full, d * C + (h - TURNED) // HG + 1)
                        nc.vector.tensor_copy(pT[:, h % TURNED, :, P:2 * P],
                                              ps[2 + (QT * h + 1) % 4][:, :]
                                              .rearrange("p (k q) -> p k q", k=KT)).then_inc(pT_dve, 1)
                    if i in SCAN_AFTER:
                        scan_one(dve, scan_group, scanned)
                dve.wait_ge(probs_ready, (d + 1) * QT * H)
                dve.wait_ge(alpha_ready, d + 1)
                fold_link(nc.vector.tensor_tensor(row_sum[:, :, :], row_sum[:, :, :], alpha[:, :, :], ALU.mult))
                fold_link(nc.vector.tensor_tensor(row_sum[:, :, :], row_sum[:, :, :], chunk_sum[:, :, :], ALU.add))
                fold_link(nc.vector.tensor_copy(m_run[:, :, :], m_new[:, :, :]))
                dve.wait_ge(alphaT_full, d + 1)
                dve.wait_ge(pv_full, (d + 1) * C)
                for b in range(2):
                    half = oT[:, 2 * b:2 * b + 2, :].rearrange("p g q -> p (g q)")
                    fold_link(nc.vector.tensor_tensor(half, half, ps[4 + b][:, :], ALU.mult))
                    fold_link(nc.vector.tensor_tensor(half, half, ps[6 + b][:, :], ALU.add))
                assert fold[0] == FOLD

            open_chunks(dve, chunk, scan_group)

            def invert_sums():
                nc.vector.reciprocal(row_inv[:, :, :], row_sum[:, :, :]).then_inc(inv_ready, 1)

            invert_sums()
            dve.wait_ge(wideT_full, 1)
            for b in range(2):
                half = oT[:, 2 * b:2 * b + 2, :].rearrange("p g q -> p (g q)")
                link(nc.vector.tensor_tensor(half, half, ps[4 + b][:, :], ALU.mult))
            for g in range(C):
                link(nc.vector.tensor_scalar(oT[:, g, :], oT[:, g, :], bias_cols[:, 2, g:g + 1], None, ALU.add))
            dve.sem_inc(oT_ready, 1)

            def add_projection(n):
                for t in range(QT):
                    dve.wait_ge(proj_full, QT * n + t + 1)
                    link(nc.vector.tensor_tensor(res[:, t, :], res[:, t, :], ps[t][:, :], ALU.add))

            add_projection(0)
            layer_norm()

            def late_wait(n):
                dve.wait_ge(tile_full, LATE + n + 1)
                return ps[n % RING]

            for t in range(QT):
                b = late_wait(t)
                dve.wait_ge(tile_act, act_took(LATE + t))
                nc.vector.tensor_tensor(xT_low[:, :, t * P:(t + 1) * P], b[:, :].rearrange("p (c q) -> p c q", c=C),
                                        xT_high[:, :, t * P:(t + 1) * P], ALU.subtract).then_inc(tile_dve, 1)
            dve.wait_ge(zeros_ready, 1)
            for g in (1, 3):
                b = late_wait(QT + g)
                for j in range(HG):
                    rows = slice(j * HEAD_DIM, (j + 1) * HEAD_DIM)
                    last = nc.vector.tensor_scalar(q2_pad[rows, HG * g + j, :], b[rows, 0:S], SCALE, None, ALU.mult)
                last.then_inc(tile_dve, 1)
            for g in (1, 3):
                b = late_wait(QT + C + g)
                nc.vector.tensor_copy(k2T[:, g, :], b[:, 0:S]).then_inc(tile_dve, 1)
            b = late_wait(QT + 2 * C + 1)
            nc.vector.tensor_copy(v[:, 1, :], b[:, :]).then_inc(tile_dve, 1)
            for i in range(H + 2):
                if i < H:
                    b = late_wait(2 * QT + 2 * C + i)
                    if i >= 3:
                        dve.wait_ge(pT2_full, i - 2)
                    p2 = probs2[:, i % 3, :]
                    nc.vector.tensor_tensor_reduce(p2[:, 0:P], b[:, 0:P], window[:, P:], 1.0, LOWEST,
                                                   ALU.add, ALU.max, m_new[:, 0, i:i + 1])
                    nc.vector.tensor_tensor_reduce(p2[:, P:], b[:, P:3 * P], window[:, :], 1.0, LOWEST,
                                                   ALU.add, ALU.max, m_new[:, 1, i:i + 1]).then_inc(tile_dve, 1)
                    dve.wait_ge(*taken(LATE + 2 * QT + 2 * C + i))
                    nc.vector.tensor_scalar(m_neg[:, :, i:i + 1], m_new[:, :, i:i + 1], -1.0, None, ALU.mult)\
                        .then_inc(neg2_ready, 1)
                if i >= 2:
                    h = i - 2
                    dve.wait_ge(pT2_full, h + 1)
                    nc.vector.tensor_copy(pT2[:, h, :], ps[4 + h % 2][:, 0:3 * P]).then_inc(pT2_taken, 1)
            dve.wait_ge(probs2_ready, H)
            invert_sums()
            for g in range(2):
                dve.wait_ge(pv2_full, 2 * g + 2)
                half = oT[:, 2 * g:2 * g + 2, :].rearrange("p g q -> p (g q)")
                link(nc.vector.tensor_copy(half, ps[6 + g][:, :]))
            dve.wait_ge(wideT_full, 2)
            for b in range(2):
                half = oT[:, 2 * b:2 * b + 2, :].rearrange("p g q -> p (g q)")
                link(nc.vector.tensor_tensor(half, half, ps[4 + b][:, :], ALU.mult))
            dve.sem_inc(oT_ready, 1)
            add_projection(1)
            layer_norm()

            dve.wait_ge(tile_full, LATE + NLATE)
            nc.vector.tensor_copy(xT[:, :, P:2 * P], ps[3][:, :].rearrange("p (c q) -> p c q", c=C))\
                .then_inc(tile_dve, 1)
            dve.wait_ge(logits_full, 1)
            logits = ps[4][:, 0:QT * E].rearrange("p (t e) -> p t e", t=QT)
            link(nc.vector.tensor_reduce(r_max[:, :, :], logits, AX.X, ALU.max))
            link(nc.vector.tensor_tensor(logit[:, :, :], logits, r_max[:, :, :].broadcast_to([P, QT, E]),
                                         ALU.subtract))
            dve.sem_inc(shift_ready, 1)
            dve.wait_ge(exp_ready, 1)
            link(nc.vector.tensor_reduce(r_sum[:, :, :], score[:, :, :], AX.X, ALU.add))
            link(nc.vector.reciprocal(r_inv[:, :, :], r_sum[:, :, :]))
            link(nc.vector.tensor_tensor(score[:, :, :], score[:, :, :], r_inv[:, :, :].broadcast_to([P, QT, E]),
                                         ALU.mult))
            for t in range(QT):
                other = score[:, t, :].unsqueeze(1).broadcast_to([P, E, E])
                own = score[:, t, :].unsqueeze(2).broadcast_to([P, E, E])
                nc.vector.tensor_tensor(above[:, t, :, :], other, own, ALU.is_gt)
                link(nc.vector.tensor_tensor(tied[:, t, :, :], other, own, ALU.is_equal))
                link(nc.vector.tensor_tensor(tied[:, t, :, :], tied[:, t, :, :], lower[:, :, :], ALU.mult))
                link(nc.vector.tensor_tensor(above[:, t, :, :], above[:, t, :, :], tied[:, t, :, :], ALU.add))
            link(nc.vector.tensor_reduce(rank[:, :, :], above[:, :, :, :], AX.X, ALU.add))
            link(nc.vector.tensor_scalar(chosen[:, :, :], rank[:, :, :], TOP_K - 0.5, None, ALU.is_lt))
            dve.sem_inc(chosen_ready, 1)

            dve.wait_ge(bias_full, 1)
            for t in range(QT):
                link(nc.vector.tensor_tensor(res[:, t, :], res[:, t, :], ps[6 + t][:, :], ALU.add))
            for n in range(QT * E):
                e, t = n // QT, n % QT
                dve.wait_ge(y_full, n + 1)
                if n >= QT:
                    dve.wait_ge(y_taken, n - QT + 1)
                nc.vector.scalar_tensor_tensor(out=res[:, t, :], in0=ps[n % 4][:, :], scalar=chosen[:, t, e:e + 1],
                                               in1=res[:, t, :], op0=ALU.mult, op1=ALU.add)\
                    .then_inc(y_taken, 1)
            for t in range(QT):
                dve.wait_ge(y_taken, QT * (E - 1) + t + 1)
                dve.sem_inc(out_ready, 1)


_INS = ['x', 'ctx_1024', 'mask_1x1xSxS2_ik0', 'L0_xattn_Wq', 'L0_xattn_bq', 'L0_xattn_Wk', 'L0_xattn_bk',
        'L0_xattn_Wv', 'L0_xattn_bv', 'L0_xattn_Wf', 'L0_xattn_bf', 'L0_attn_Wq', 'L0_attn_Wk', 'L0_attn_Wv',
        'L0_attn_Wo', 'L0_ffn_weight', 'L0_ffn_bias', 'L0_ffn_router_weight', 'L0_ffn_router_bias']


def kernel(**inputs):
    import numpy as np
    import concourse.bacc as bacc
    from concourse.bass_utils import run_bass_kernel_spmd

    nc = bacc.Bacc("TRN2", target_bir_lowering=False, num_devices=1)
    arrays, args = {}, []
    for name in _INS:
        a = np.ascontiguousarray(inputs[name])
        arrays[f"in_{name}"] = a
        args.append(nc.dram_tensor(f"in_{name}", a.shape, mybir.dt.from_np(a.dtype), kind="ExternalInput").ap())
    out = nc.dram_tensor("out_x", inputs['x'].shape, F32, kind="ExternalOutput").ap()
    build_perceiver(nc, *args, out)
    r = run_bass_kernel_spmd(nc, [arrays], core_ids=[0])
    return r.results[0]["out_x"]
```

```python
from contextlib import ExitStack

import concourse.bass as bass
from concourse import mybir

F32 = mybir.dt.float32
BF16 = mybir.dt.bfloat16
I32 = mybir.dt.int32
ALU = mybir.AluOpType
ACT = mybir.ActivationFunctionType
AX = mybir.AxisListType

P = 128
BANK = 512
HEAD_DIM = 32
LN_EPS = 1e-5
MASKED = -1e30
LOWEST = -3e38
TOP_K = 2


def build_perceiver(nc, x, ctx, mask, wq, bq, wk, bk, wv, bv, wf, bf, awq, awk, awv, awo,
                    ffn_w, ffn_b, router_w, router_b, out):
    _, S, D = x.shape
    KEYS = ctx.shape[1]
    E = ffn_w.shape[0]
    H = D // HEAD_DIM
    SCALE = float(HEAD_DIM) ** -0.5
    QT = S // P
    C = D // P
    HG = P // HEAD_DIM
    CHUNK = BANK
    KT = CHUNK // P
    NCHUNK = KEYS // CHUNK
    GROUP = 7
    NGROUP = NCHUNK // GROUP
    PIECE = GROUP * CHUNK
    ACT_CHUNKS = 3
    assert QT == 2 and C == 4 and NGROUP * GROUP == NCHUNK and NCHUNK * CHUNK == KEYS and E == 8

    weights = [wq, wk, wv, awq, awk, awv, wf, awo]
    WQ, WK, WV, AWQ, AWK, AWV, WF, AWO = range(8)
    SLOT = {WQ: 0, WF: 1, AWO: 0}
    PAIR = {WK: 0, WV: 1, AWQ: 2, AWK: 3, AWV: 4}
    NSTAGE = 3
    EARLY_SCANS = {WV: 0}
    NEARLY = len(EARLY_SCANS)
    SCAN_AFTER = (-1, 3, 8)
    WEIGH_AFTER = ((7, 8, 8, 9), (10, 11, 12, 12), (14, 15, 16, 16), (18, 18, 18, 18))
    TURNED = 8

    mask_q = mask.rearrange("a b (t p) k -> p (a b t) k", p=P)
    ctx_k = ctx.rearrange("a k d -> (a k) d")

    with ExitStack() as es:
        def sb(name, shape, dt=F32):
            return es.enter_context(nc.sbuf_tensor(name, shape, dt))

        def sem(name):
            return es.enter_context(nc.semaphore(name))

        def pair(name, shape):
            return sb(name + "_high", shape, BF16), sb(name + "_low", shape, BF16)

        ident = sb("ident", [P, P])
        ones_row = sb("ones_row", [1, P])
        bit_weight = sb("bit_weight", [1, GROUP])
        window = sb("window", [P, 2 * P])
        lower = sb("lower", [P, E, E])
        stage = sb("stage", [P, NSTAGE, C, D])
        wT = sb("wT", [P, 2, C, D])
        wT_high, wT_low = pair("wT", [P, 5, C, D])
        q2_pad = sb("q2_pad", [P, H, S])
        scan_flat = q2_pad[:, :, :].rearrange("p h q -> p (h q)")[:, 0:QT * PIECE // 2]
        scan = scan_flat.bitcast(BF16).rearrange("p (t k) -> p t k", t=QT)
        scan_pairs = scan_flat.bitcast(I32).rearrange("p (t k) -> p t k", t=QT)
        pT_all = sb("pT_all", [P, TURNED * KT * S])
        pT = pT_all[:, :].rearrange("p (b k q) -> p b k q", b=TURNED, k=KT)
        pT2 = pT_all[:, 0:H * 3 * P].rearrange("p (h k) -> p h k", h=H)
        probs_all = sb("probs_all", [P, 3 * QT * CHUNK])
        probs = probs_all[:, :].rearrange("p (b t k) -> p b t k", b=3, t=QT)
        probs2 = probs_all[:, 0:3 * 3 * P].rearrange("p (b k) -> p b k", b=3)
        LATE_HEADS = 6 * KT * S
        q_full = probs_all[:, 0:C * S].rearrange("p (g q) -> p g q", g=C)
        q_high = pT_all[:, LATE_HEADS:LATE_HEADS + C * S // 2].bitcast(BF16).rearrange("p (g q) -> p g q", g=C)
        q_low = pT_all[:, LATE_HEADS + C * S // 2:LATE_HEADS + C * S].bitcast(BF16).rearrange("p (g q) -> p g q", g=C)
        q_stack = sb("q_stack", [P, H, S], BF16)
        stage_flat = stage[:, :, :, :].rearrange("p b c d -> p (b c d)")
        k_stack = stage_flat[:, 0:H * CHUNK // 2].bitcast(BF16)\
            .rearrange("p (h k) -> p h k", h=H)
        q_pad = stage_flat[:, 0:HG * S].bitcast(BF16).rearrange("p (j i q) -> p j i q", j=HG, i=2)
        ctx_in = stage_flat[:, H * CHUNK // 2:].rearrange("p (t d) -> p t d", t=KT)
        ctxT_high, ctxT_low = pair("ctxT", [P, C, CHUNK])
        kT_all = sb("kT_all", [P, 2, C * CHUNK // 2])
        kT_high = kT_all[:, 0, :].bitcast(BF16).rearrange("p (c k) -> p c k", c=C)
        kT_low = kT_all[:, 1, :].bitcast(BF16).rearrange("p (c k) -> p c k", c=C)
        k2T = kT_all[:, 0, :].rearrange("p (c k) -> p c k", c=C)
        v = sb("v", [P, KT, D])
        mask_in = sb("mask_in", [P, QT, CHUNK], I32)
        mask_add = sb("mask_add", [P, QT, CHUNK])
        oT = sb("oT", [P, C, S])
        res = sb("res", [P, QT, D])
        xn = mask_add
        xT = sb("xT", [P, C, S])
        xT_high = xT[:, 0:2, :].rearrange("p c s -> p (c s)").bitcast(BF16).rearrange("p (c s) -> p c s", c=C)
        xT_low = xT[:, 2:4, :].rearrange("p c s -> p (c s)").bitcast(BF16).rearrange("p (c s) -> p c s", c=C)
        ln_stats = sb("ln_stats", [P, QT, 6])
        ln_mv = sb("ln_mv", [P, QT, 2])
        ln_rstd = sb("ln_rstd", [P, QT, 1])
        bias_rows = sb("bias_rows", [3 * C, P])
        bias_cols = sb("bias_cols", [P, 3, C])
        bf_row = sb("bf_row", [1, D])
        rb_row = sb("rb_row", [1, E])
        ffn_b_sb = sb("ffn_b_sb", [E, D])
        rw_rows = sb("rw_rows", [E, D])
        rwT = sb("rwT", [P, C, E])
        open_size = sb("open_size", [P, QT, GROUP])
        is_open = sb("is_open", [P, QT, GROUP])
        open_count = sb("open_count", [P, QT, GROUP + 1])
        flag = sb("flag", [P, QT, GROUP])
        bits = sb("bits", [1, GROUP + 1])
        row_shut = sb("row_shut", [P, QT])
        shut_flag = sb("shut_flag", [P, QT])
        word_of = sb("word_of", [1, NGROUP])
        any_left = sb("any_left", [1, 1])
        first_word = sb("first_word", [1, 1], I32)
        left_word = sb("left_word", [1, 1], I32)
        rest_words = sb("rest_words", [1, 2 * NGROUP], I32)
        table_use = sb("table_use", [1, 4])
        gate = sb("gate", [P, QT, H])
        m_run = sb("m_run", [P, QT, H])
        m_new = sb("m_new", [P, QT, H])
        m_neg = sb("m_neg", [P, QT, H])
        m_diff = sb("m_diff", [P, QT, H])
        alpha = sb("alpha", [P, QT, H])
        chunk_sum = sb("chunk_sum", [P, QT, H])
        row_sum = sb("row_sum", [P, QT, H])
        row_inv = sb("row_inv", [P, QT, H])
        logit = sb("logit", [P, QT, E])
        r_max = sb("r_max", [P, QT, 1])
        score = sb("score", [P, QT, E])
        r_sum = sb("r_sum", [P, QT, 1])
        r_inv = sb("r_inv", [P, QT, 1])
        above = v[:, 0, 0:QT * E * E].rearrange("p (t e f) -> p t e f", t=QT, e=E)
        tied = v[:, 1, 0:QT * E * E].rearrange("p (t e f) -> p t e f", t=QT, e=E)
        chosenT = v[0:E, 2, 0:QT * P].rearrange("e (t q) -> e t q", t=QT)
        rank = sb("rank", [P, QT, E])
        chosen = sb("chosen", [P, QT, E])
        ps = [es.enter_context(nc.psum_tensor(f"bank{i}", [P, BANK], F32)) for i in range(8)]

        x_loaded = sem("x_loaded")
        small_loaded = sem("small_loaded")
        stage_loaded = [sem(f"stage_loaded{i}") for i in range(NSTAGE)]
        scan_loaded = sem("scan_loaded")
        q_stacked = sem("q_stacked")
        pad_cleared = sem("pad_cleared")
        q_padded = sem("q_padded")
        k_stacked = [sem(f"k_stacked{i}") for i in range(2)]
        ctx_loaded = sem("ctx_loaded")
        mask_loaded = sem("mask_loaded")
        out_stored = sem("out_stored")
        pool_step = sem("pool_step")
        consts_ready = sem("consts_ready")
        dve_step = sem("dve_step")
        var_ready = sem("var_ready")
        std_ready = sem("std_ready")
        norm_ready = sem("norm_ready")
        tile_full = sem("tile_full")
        tile_act = sem("tile_act")
        tile_dve = sem("tile_dve")
        scan_act = sem("scan_act")
        scan_dve = sem("scan_dve")
        q_full_ready = sem("q_full_ready")
        q_high_ready = sem("q_high_ready")
        q_low_ready = sem("q_low_ready")
        size_used = sem("size_used")
        first_word_ready = sem("first_word_ready")
        rest_words_ready = sem("rest_words_ready")
        zeros_ready = sem("zeros_ready")
        ctx_turned = sem("ctx_turned")
        mask_used = sem("mask_used")
        ring_full = sem("ring_full")
        ring_act = sem("ring_act")
        ring_dve = sem("ring_dve")
        neg_ready = sem("neg_ready")
        probs_ready = sem("probs_ready")
        pT_full = sem("pT_full")
        pT_act = sem("pT_act")
        pT_dve = sem("pT_dve")
        pv_full = sem("pv_full")
        diff_ready = sem("diff_ready")
        alpha_ready = sem("alpha_ready")
        alpha_spread = sem("alpha_spread")
        fold_step = sem("fold_step")
        neg2_ready = sem("neg2_ready")
        probs2_ready = sem("probs2_ready")
        pT2_full = sem("pT2_full")
        pT2_taken = sem("pT2_taken")
        pv2_full = sem("pv2_full")
        inv_ready = sem("inv_ready")
        inv_spread = sem("inv_spread")
        oT_ready = sem("oT_ready")
        proj_full = sem("proj_full")
        logits_full = sem("logits_full")
        shift_ready = sem("shift_ready")
        exp_ready = sem("exp_ready")
        chosen_ready = sem("chosen_ready")
        chosenT_full = sem("chosenT_full")
        chosenT_ready = sem("chosenT_ready")
        bias_full = sem("bias_full")
        y_full = sem("y_full")
        y_taken = sem("y_taken")
        out_ready = sem("out_ready")

        setup_tiles = [("x", 0), ("x", 1), ("small", 0)]
        setup_tiles += [("w", (WQ, o)) for o in range(C)] + [("q", g) for g in range(C)]
        for w in range(1, 8):
            setup_tiles += [("w", (w, o)) for o in range(C)]

        def taker(n, kind, a):
            if kind in ("q", "small"):
                return "dve"
            if kind == "w" and a[0] in PAIR:
                return "both"
            return "dve" if n % 2 else "act"

        takers = [taker(n, kind, a) for n, (kind, a) in enumerate(setup_tiles)]
        NSETUP = len(setup_tiles)
        w_tile = {a: n for n, (kind, a) in enumerate(setup_tiles) if kind == "w"}
        q_tile = [n for n, (kind, _) in enumerate(setup_tiles) if kind == "q"]
        LATE = NSETUP
        takers += ["both"] * QT + ["act", "dve"] * (C + QT // 2) + ["dve"] * H + ["act", "dve"]
        NLATE = len(takers) - LATE
        RING = 4

        def act_took(n):
            return takers[:n + 1].count("act") + takers[:n + 1].count("both")

        def dve_took(n):
            return takers[:n + 1].count("dve") + takers[:n + 1].count("both")

        def taken(n):
            return (tile_act, act_took(n)) if takers[n] == "act" else (tile_dve, dve_took(n))

        BETWEEN = {0: ("k", 2, 6), 1: ("v", 0, 7), 2: ("v", 1, 6), 3: ("k", 3, 7), 4: ("v", 2, 6), 5: ("v", 3, 7)}
        BANK_OF = {("k", 0): 2, ("k", 1): 3}
        BANK_OF.update({(kind, n): b for kind, n, b in BETWEEN.values()})
        tensor_order = [("ctx", k) for k in range(KT)] + [("k", 0), ("k", 1)]
        vector_order = list(tensor_order)
        for h in range(H):
            tensor_order += [("score", QT * h + t) for t in range(QT)]
            vector_order += [("score", QT * h + t) for t in range(QT)]
            if h in BETWEEN:
                tensor_order.append(BETWEEN[h][:2])
            if h - 1 in BETWEEN:
                vector_order.append(BETWEEN[h - 1][:2])

        def act_takes(tile):
            return tile[0] in ("ctx", "k") or tile[0] == "v" and tile[1] % 2 == 0

        def dve_takes(tile):
            return tile[0] in ("ctx", "k", "score") or tile[0] == "v" and tile[1] % 2 == 1

        def place(order, tile, counted):
            return sum(1 for other in order[:order.index(tile) + 1] if counted(other))

        RING_ACT = sum(1 for tile in tensor_order if act_takes(tile))
        RING_DVE = sum(1 for tile in tensor_order if dve_takes(tile))
        NFULL = len(tensor_order) - KT
        NSTACK = 4 * HG
        FOLD = 9

        def by_act(tile, d):
            return ring_act, d * RING_ACT + place(tensor_order, tile, act_takes)

        def by_dve(tile, d):
            return ring_dve, ONE + d * RING_DVE + place(vector_order, tile, dve_takes)

        def taken_in(tile, d):
            return by_dve(tile, d) if dve_takes(tile) else by_act(tile, d)

        def full(tile, d):
            return ring_full, ONE + d * NFULL + place(tensor_order, tile, lambda other: other[0] != "ctx")

        ONE = 1
        NCONST = 4 + 1 + GROUP + 3

        def scan_one(eng, scan, scanned):
            with eng.If(eng.snap(scanned) != NGROUP):
                scan(eng.snap(scanned, min_val=NEARLY, max_val=NGROUP - 1))
                eng.reg_add(scanned, scanned, 1)

        def open_chunks(eng, body, scan=None):
            done = eng.alloc_register("chunks_done")
            scanned = eng.alloc_register("groups_scanned")
            word = eng.alloc_register("chunk_word")
            first = eng.alloc_register("first_chunk")

            def group():
                with eng.Fori(0, GROUP) as j:
                    with eng.If((eng.snap(word) & 1) != 0):
                        body(eng.snap(first, min_val=0, max_val=NCHUNK - GROUP) + j,
                             eng.snap(done, min_val=0, max_val=NCHUNK - 1), scanned)
                        eng.reg_add(done, done, 1)
                    eng.reg_alu(word, word, 1, op=ALU.logical_shift_right)

            eng.reg_mov(done, 0)
            eng.reg_mov(scanned, NEARLY)
            eng.reg_mov(first, NCHUNK - GROUP)
            eng.wait_ge(first_word_ready, 1)
            eng.reg_mov(word, eng.value_load(first_word[0:1, 0:1], min_val=0, max_val=2 ** GROUP - 1))
            group()
            if scan is not None:
                with eng.If(eng.snap(scanned) != NGROUP):
                    with eng.Fori(0, NGROUP - NEARLY):
                        scan_one(eng, scan, scanned)
            eng.wait_ge(rest_words_ready, 1)
            with eng.If(eng.value_load(left_word[0:1, 0:1], min_val=0, max_val=1) != 0):
                with eng.Fori(0, 2) as shut:
                    eng.reg_mov(first, NCHUNK - GROUP)
                    with eng.Fori(0, NGROUP) as g:
                        eng.reg_mov(word, eng.value_load(rest_words[0:1, bass.ds(shut * NGROUP + g, 1)], min_val=0,
                                                         max_val=2 ** GROUP - 1))
                        with eng.If(eng.snap(word) != 0):
                            group()
                        eng.reg_sub(first, first, GROUP)

        block = es.enter_context(nc.Block())

        @block.sync
        def _(sp):
            def load_weight(w):
                sp.dma_start(stage[:, w % NSTAGE, :, :], weights[w].rearrange("(o p) c -> p o c", p=P))\
                    .then_inc(stage_loaded[w % NSTAGE], 16)

            def load_expert(e):
                n = 8 + e
                sp.dma_start(stage[:, n % NSTAGE, :, :], ffn_w[e].rearrange("(c p) k -> p c k", p=P))\
                    .then_inc(stage_loaded[n % NSTAGE], 16)

            sp.dma_start(res[:, :, :], x.rearrange("a (t p) d -> p (a t) d", p=P)).then_inc(x_loaded, 16)
            for w in range(8):
                if w >= NSTAGE:
                    sp.wait_ge(tile_full, w_tile[(w - NSTAGE, C - 1)] + 1)
                load_weight(w)
            assert AWV % NSTAGE == 2

            def load_chunk(c, d, scanned):
                first = sp.snap(c * CHUNK)
                sp.wait_ge(tile_full, w_tile[(AWV, C - 1)] + 1)
                sp.wait_ge(mask_used, ONE + d)
                sp.wait_ge(ctx_turned, ONE + d * KT)
                sp.dma_start(ctx_in, ctx_k[bass.ds(first, CHUNK), :]
                             .rearrange("(t p) d -> p t d", p=P)).then_inc(ctx_loaded, 16)
                sp.dma_start(mask_in[:, :, :], mask_q[:, :, bass.ds(first, CHUNK)])\
                    .then_inc(mask_loaded, 16)
                stacked = k_stack.rearrange("p (g j) k -> p g j k", j=HG)
                for i, (low_g, high_g) in enumerate(((1, 2), (2, 4))):
                    for part, kT_part in enumerate((kT_high, kT_low)):
                        if i == part == 0:
                            sp.wait_ge(ring_full, ONE + d * NFULL)
                        sp.wait_ge(*(by_act, by_dve)[part](("k", high_g - 1), d))
                        for j in range(HG):
                            for slot in (2 * part, 2 * part + 1):
                                sp.dma_start(stacked[slot * HEAD_DIM:(slot + 1) * HEAD_DIM, low_g:high_g, j, :],
                                             kT_part[j * HEAD_DIM:(j + 1) * HEAD_DIM, low_g:high_g, :])\
                                    .then_inc(k_stacked[i], 16)

            open_chunks(sp, load_chunk)
            sp.wait_ge(inv_spread, 2)
            for e in range(E):
                if e >= NSTAGE:
                    sp.wait_ge(y_full, QT * (e - NSTAGE + 1))
                load_expert(e)
            out_q = out.rearrange("a (t p) d -> p (a t) d", p=P)
            for t in range(QT):
                sp.wait_ge(out_ready, t + 1)
                sp.dma_start(out_q[:, t, :], res[:, t, :]).then_inc(out_stored, 16)
            sp.wait_ge(out_stored, 16 * QT)

        @block.gpsimd
        def _(pool):
            def load_group(g):
                first = (NGROUP - 1 - g) * PIECE
                for t in range(QT):
                    pool.dma_start(scan[:, t, :], mask_q[:, t, first:first + PIECE]).then_inc(scan_loaded, 16)

            pool.sem_inc(size_used, ONE)
            nc.gpsimd.memset(ident[:, :], 0.0).then_inc(pool_step, 1)
            nc.gpsimd.memset(window[:, :], 0.0).then_inc(pool_step, 1)
            nc.gpsimd.memset(lower[:, :, :], 1.0).then_inc(pool_step, 1)
            nc.gpsimd.memset(bits[:, :], 0.0).then_inc(pool_step, 1)
            nc.gpsimd.memset(open_count[:, :, :], 0.0).then_inc(pool_step, 1)
            nc.gpsimd.memset(word_of[:, :], 0.0).then_inc(pool_step, 1)
            nc.gpsimd.memset(any_left[:, :], 0.0).then_inc(pool_step, 1)
            pool.wait_ge(pool_step, 7)
            nc.gpsimd.affine_select(out=ident[:, :], in_=ident[:, :], compare_op=ALU.not_equal, fill=1.0,
                                    base=0, pattern=[[-1, P]], channel_multiplier=1).then_inc(consts_ready, 1)
            pool.wait_ge(stage_loaded[WK], 16)
            load_group(0)
            nc.gpsimd.affine_select(out=window[:, 0:P], in_=window[:, 0:P], compare_op=ALU.is_ge, fill=MASKED,
                                    base=-1, pattern=[[1, P]], channel_multiplier=-1).then_inc(consts_ready, 1)
            nc.gpsimd.affine_select(out=window[:, P:], in_=window[:, P:], compare_op=ALU.is_ge, fill=MASKED,
                                    base=0, pattern=[[-1, P]], channel_multiplier=1).then_inc(consts_ready, 1)
            nc.gpsimd.affine_select(out=lower[:, :, :], in_=lower[:, :, :], compare_op=ALU.is_ge, fill=0.0,
                                    base=-1, pattern=[[1, E], [-1, E]], channel_multiplier=0)\
                .then_inc(consts_ready, 1)
            nc.gpsimd.memset(ones_row[:, :], 1.0).then_inc(consts_ready, 1)
            for j in range(GROUP):
                nc.gpsimd.memset(bit_weight[:, j:j + 1], float(2 ** j)).then_inc(consts_ready, 1)
            nc.gpsimd.memset(oT[:, :, :], 0.0).then_inc(consts_ready, 1)
            nc.gpsimd.memset(m_run[:, :, :], LOWEST).then_inc(consts_ready, 1)
            nc.gpsimd.memset(row_sum[:, :, :], 0.0).then_inc(consts_ready, 1)
            pool.wait_ge(consts_ready, NCONST)

            steps = [7]

            def link(ins):
                steps[0] += 1
                ins.then_inc(pool_step, 1)
                pool.wait_ge(pool_step, steps[0])

            for g in range(NGROUP):
                pool.wait_ge(scan_act, g + 1)
                pool.wait_ge(scan_dve, g + 1)
                link(nc.gpsimd.tensor_scalar(is_open[:, :, :], open_size[:, :, :], 0.0, None, ALU.is_gt))
                pool.sem_inc(size_used, 1)
                if 0 < g < NGROUP - 1:
                    load_group(g + 1)
                link(nc.gpsimd.tensor_tensor(open_count[:, :, 0:GROUP], open_count[:, :, 0:GROUP], is_open[:, :, :],
                                             ALU.add))
                link(nc.gpsimd.partition_all_reduce(flag[:, :, :].rearrange("p t j -> p (t j)"),
                                                    is_open[:, :, :].rearrange("p t j -> p (t j)"), P,
                                                    bass.bass_isa.ReduceOp.max))
                link(nc.gpsimd.tensor_tensor(bits[:, 0:GROUP], flag[0:1, 0, :], flag[0:1, 1, :], ALU.add))
                link(nc.gpsimd.tensor_scalar(bits[:, 0:GROUP], bits[:, 0:GROUP], 0.0, None, ALU.is_gt))
                link(nc.gpsimd.tensor_tensor(bits[:, 0:GROUP], bits[:, 0:GROUP], bit_weight[:, :], ALU.mult))
                for half in (4, 2, 1):
                    link(nc.gpsimd.tensor_tensor(bits[:, 0:half], bits[:, 0:half], bits[:, half:2 * half], ALU.add))
                if g == 0:
                    nc.gpsimd.tensor_copy(first_word[:, :], bits[:, 0:1]).then_inc(first_word_ready, 1)
                    pool.wait_ge(tile_full, max(w_tile[(w, C - 1)] for w in range(8) if w % NSTAGE == 0) + 1)
                    nc.gpsimd.memset(q_pad[:, :, :, :], 0.0).then_inc(pad_cleared, 1)
                    pool.wait_ge(stage_loaded[AWO % NSTAGE], 16 * (AWO // NSTAGE + 1))
                    load_group(1)
                    stacked_q = q_stack[:, :, :].rearrange("p (g j) q -> p g j q", j=HG)
                    pool.wait_ge(q_high_ready, 1)
                    pool.wait_ge(q_low_ready, 1)
                    for j in range(HG):
                        for slot in range(4):
                            pool.dma_start(stacked_q[slot * HEAD_DIM:(slot + 1) * HEAD_DIM, :, j, :],
                                           (q_high, q_low)[slot % 2][j * HEAD_DIM:(j + 1) * HEAD_DIM, :, :])\
                                .then_inc(q_stacked, 16)
                else:
                    link(nc.gpsimd.tensor_tensor(any_left[:, :], any_left[:, :], bits[:, 0:1], ALU.add))
                    link(nc.gpsimd.tensor_copy(word_of[:, g:g + 1], bits[:, 0:1]))
            link(nc.gpsimd.tensor_copy(rest_words[:, 0:NGROUP], word_of[:, :]))
            link(nc.gpsimd.tensor_copy(word_of[:, 0:1], first_word[:, :]))
            link(nc.gpsimd.tensor_scalar(word_of[:, :], word_of[:, :], -1.0, 2.0 ** GROUP - 1.0, ALU.mult, ALU.add))
            for half in (4, 2, 1):
                link(nc.gpsimd.tensor_tensor(open_count[:, :, 0:half], open_count[:, :, 0:half],
                                             open_count[:, :, half:2 * half], ALU.add))
            link(nc.gpsimd.tensor_scalar(row_shut[:, :], open_count[:, :, 0], 0.0, None, ALU.is_equal))
            link(nc.gpsimd.partition_all_reduce(shut_flag[:, :], row_shut[:, :], P, bass.bass_isa.ReduceOp.max))
            link(nc.gpsimd.tensor_tensor(bits[:, 0:1], shut_flag[0:1, 0:1], shut_flag[0:1, 1:2], ALU.add))
            link(nc.gpsimd.tensor_scalar(bits[:, 0:1], bits[:, 0:1], 0.0, None, ALU.is_gt))
            link(nc.gpsimd.tensor_tensor(word_of[:, :], word_of[:, :], bits[:, 0:1].broadcast_to([1, NGROUP]),
                                         ALU.mult))
            link(nc.gpsimd.tensor_copy(rest_words[:, NGROUP:2 * NGROUP], word_of[:, :]))
            link(nc.gpsimd.tensor_tensor(any_left[:, :], any_left[:, :], bits[:, 0:1], ALU.add))
            link(nc.gpsimd.tensor_scalar(any_left[:, :], any_left[:, :], 0.0, None, ALU.is_gt))
            nc.gpsimd.tensor_copy(left_word[:, :], any_left[:, :]).then_inc(rest_words_ready, 1)
            nc.gpsimd.memset(q2_pad[:, :, :], 0.0).then_inc(zeros_ready, 1)

        @block.tensor
        def _(pe):
            def spread(a, half_full):
                for g in range(C):
                    for t in range(QT):
                        at = (g % 2) * S + t * P
                        for j in range(HG):
                            rows = slice(j * HEAD_DIM, (j + 1) * HEAD_DIM)
                            h = HG * g + j
                            last = nc.tensor.matmul(ps[4 + g // 2][rows, at:at + P],
                                                    a[:, t, h:h + 1].broadcast_to([P, HEAD_DIM]), ident[:, :],
                                                    start=True, stop=True, tile_position=(0, j * HEAD_DIM))
                    if g % 2:
                        last.then_inc(half_full, 1)

            def transpose(o, i, n=P):
                return nc.tensor.transpose(o, i, ident[0:n, 0:n])

            def setup_tile(n):
                kind, a = setup_tiles[n]
                if n >= 8:
                    pe.wait_ge(*taken(n - 8))
                b = ps[n % 8]
                if kind == "x":
                    pe.wait_ge(norm_ready, a + 1)
                    for c in range(C):
                        last = transpose(b[:, c * P:(c + 1) * P], xn[:, a, c * P:(c + 1) * P])
                elif kind == "small":
                    pe.wait_ge(small_loaded, 16 * 7)
                    transpose(b[:, 0:3 * C], bias_rows[:, :], 3 * C)
                    for c in range(C):
                        last = transpose(b[:, 64 + c * E:64 + (c + 1) * E], rw_rows[:, c * P:(c + 1) * P], E)
                elif kind == "w":
                    w, o = a
                    pe.wait_ge(stage_loaded[w % NSTAGE], 16 * (w // NSTAGE + 1))
                    for c in range(C):
                        last = transpose(b[:, c * P:(c + 1) * P], stage[:, w % NSTAGE, o, c * P:(c + 1) * P])
                else:
                    if a == 0:
                        pe.wait_ge(*taken(0))
                        pe.wait_ge(*taken(1))
                        pe.wait_ge(*taken(w_tile[(WQ, C - 2)]))
                        pe.wait_ge(*taken(w_tile[(WQ, C - 1)]))
                    for c in range(C):
                        last = nc.tensor.matmul(b[:, 0:S], wT[:, SLOT[WQ], c, a * P:(a + 1) * P], xT[:, c, :],
                                                start=(c == 0), stop=(c == C - 1))
                last.then_inc(tile_full, 1)

            pe.sem_inc(ctx_turned, ONE)
            pe.sem_inc(pT_full, ONE)
            pe.sem_inc(ring_full, ONE)
            pe.wait_ge(consts_ready, NCONST)
            for n in range(NSETUP):
                setup_tile(n)
            pe.wait_ge(tile_act, act_took(NSETUP - 1))
            pe.wait_ge(tile_dve, dve_took(NSETUP - 1))

            def products(b, stationary, moving):
                terms = [(c, i, j) for c in range(C) for i, j in ((0, 0), (0, 1), (1, 0))]
                for n, (c, i, j) in enumerate(terms):
                    last = nc.tensor.matmul(b, stationary(i, c), moving(j, c), start=(n == 0),
                                            stop=(n == len(terms) - 1))
                return last

            wT_parts = (wT_high, wT_low)
            ctxT_parts = (ctxT_high, ctxT_low)
            xT_parts = (xT_high, xT_low)

            def chunk(c, d, scanned):
                def project_k(g, b):
                    products(b[:, :], lambda i, cc: wT_parts[i][:, PAIR[WK], cc, g * P:(g + 1) * P],
                             lambda i, cc: ctxT_parts[i][:, cc, :]).then_inc(ring_full, 1)

                def project_v(k, b):
                    products(b[:, :], lambda i, cc: ctxT_parts[i][:, cc, k * P:(k + 1) * P],
                             lambda i, cc: wT_parts[i][:, PAIR[WV], cc, :]).then_inc(ring_full, 1)

                for k in range(KT):
                    if k == 0:
                        pe.wait_ge(ring_dve, ONE + d * RING_DVE)
                        pe.wait_ge(ctx_loaded, d * 16 + 16)
                    for cc in range(C):
                        last = transpose(ps[k][:, cc * P:(cc + 1) * P], ctx_in[:, k, cc * P:(cc + 1) * P])
                    last.then_inc(ctx_turned, 1)
                pe.wait_ge(*taken_in(("ctx", KT - 1), d))
                for g in range(2):
                    project_k(g, ps[BANK_OF[("k", g)]])

                def project_between(i):
                    kind, n, bank = BETWEEN[i]
                    if i == 0:
                        pe.wait_ge(fold_step, ONE + d * FOLD)
                    elif i >= 2:
                        pe.wait_ge(*taken_in(BETWEEN[i - 2][:2], d))
                    (project_k if kind == "k" else project_v)(n, ps[bank])

                def scores(h):
                    for t in range(QT):
                        if h == 0 and t == 0:
                            pe.wait_ge(*taken_in(("k", 0), d))
                        elif h > 0:
                            pe.wait_ge(*taken_in(("score", QT * (h - 1) + t), d))
                        if h == t == 0:
                            pe.wait_ge(q_padded, 2 * HG)
                        if h == HG and t == 0:
                            pe.wait_ge(q_stacked, 16 * NSTACK)
                        if t == 0 and h in (HG, 2 * HG):
                            pe.wait_ge(k_stacked[h // HG - 1], (d + 1) * 16 * NSTACK)
                        if h < HG:
                            for n, (q_part, kT_part) in enumerate(((0, kT_high), (1, kT_high), (0, kT_low))):
                                last = nc.tensor.matmul(ps[t][:, :], q_pad[:, h, q_part, t * P:(t + 1) * P],
                                                        kT_part[:, 0, :], start=(n == 0), stop=(n == 2))
                        else:
                            last = nc.tensor.matmul(ps[t][:, :], q_stack[:, h, t * P:(t + 1) * P], k_stack[:, h, :],
                                                    start=True, stop=True)
                        last.then_inc(ring_full, 1)

                def turn_probs(h):
                    for t in range(QT):
                        m = QT * h + t
                        pe.wait_ge(probs_ready, d * QT * H + m + 1)
                        if h >= 2:
                            pe.wait_ge(pT_act if t == 0 else pT_dve, d * H + h - 1)
                        elif h == 0:
                            pe.wait_ge(*taken_in(("k", t), d))
                        b = ps[2 + m % 4]
                        for k in range(KT):
                            last = transpose(b[:, k * P:(k + 1) * P], probs[:, h % 3, t, k * P:(k + 1) * P])
                        last.then_inc(pT_full, 1)

                def weigh_values(g, k):
                    if k == 0:
                        pe.wait_ge(pT_act, d * H + HG * (g + 1))
                        pe.wait_ge(pT_dve, d * H + HG * (g + 1))
                    if g == C - 1 and k == 0:
                        pe.wait_ge(alpha_ready, d + 1)
                        spread(alpha, alpha_spread)
                    if g == k == 0:
                        pe.wait_ge(*taken_in(("v", KT - 2), d))
                        pe.wait_ge(*taken_in(("v", KT - 1), d))
                    b = ps[6 + g // 2]
                    for j in range(HG):
                        h = HG * g + j
                        rows = slice(j * HEAD_DIM, (j + 1) * HEAD_DIM)
                        last = nc.tensor.matmul(b[rows, (g % 2) * S:(g % 2 + 1) * S],
                                                v[:, k, h * HEAD_DIM:(h + 1) * HEAD_DIM],
                                                pT[:, h % TURNED, k, :], start=(k == 0), stop=(k == KT - 1),
                                                tile_position=(0, j * HEAD_DIM))
                    if k == KT - 1:
                        last.then_inc(pv_full, 1)

                for i in range(H + 3):
                    if i < H:
                        scores(i)
                    if i in BETWEEN:
                        project_between(i)
                    if 2 <= i < H + 2:
                        turn_probs(i - 2)
                    for g, steps in enumerate(WEIGH_AFTER):
                        for k in range(KT):
                            if steps[k] == i:
                                weigh_values(g, k)

            open_chunks(pe, chunk)

            def project(w, n, bias_row=None):
                if bias_row is not None:
                    for t in range(QT):
                        nc.tensor.matmul(ps[t][:, :], ones_row[:, :], bias_row[:, :], start=True, stop=False)
                for t in range(QT):
                    for g in range(C):
                        if t == 0 and g % 2 == 0:
                            pe.wait_ge(oT_ready, 2 * (n - 1) + g // 2 + 1)
                        last = nc.tensor.matmul(ps[t][:, :], oT[:, g, t * P:(t + 1) * P], wT[:, SLOT[w], g, :],
                                                start=(g == 0 and bias_row is None), stop=(g == C - 1))
                    last.then_inc(proj_full, 1)

            pe.wait_ge(inv_ready, 1)
            spread(row_inv, inv_spread)
            project(WF, 1, bf_row)

            def late(n):
                if n >= RING:
                    pe.wait_ge(*taken(LATE + n - RING))
                return ps[n % RING]

            def late_wait(n):
                pe.wait_ge(*taken(LATE + n))

            for t in range(QT):
                b = late(t)
                pe.wait_ge(norm_ready, QT + t + 1)
                for c in range(C):
                    last = transpose(b[:, c * P:(c + 1) * P], xn[:, t, c * P:(c + 1) * P])
                last.then_inc(tile_full, 1)
            late_wait(0)
            late_wait(1)
            for i, w in enumerate((AWQ, AWK)):
                for g in range(C):
                    b = late(QT + C * i + g)
                    products(b[:, 0:S], lambda i, c: wT_parts[i][:, PAIR[w], c, g * P:(g + 1) * P],
                             lambda i, c: xT_parts[i][:, c, :]).then_inc(tile_full, 1)
            for t in range(QT):
                b = late(QT + 2 * C + t)
                products(b[:, :], lambda i, c: xT_parts[i][:, c, t * P:(t + 1) * P],
                         lambda i, c: wT_parts[i][:, PAIR[AWV], c, :]).then_inc(tile_full, 1)

            def scores2(h):
                b = late(2 * QT + 2 * C + h)
                if h % HG == 0:
                    late_wait(QT + h // HG)
                    late_wait(QT + C + h // HG)
                k2 = k2T[:, h // HG, :]
                nc.tensor.matmul(b[:, 0:P], q2_pad[:, h, 0:P], k2[:, 0:P], start=True, stop=True)
                nc.tensor.matmul(b[:, P:3 * P], q2_pad[:, h, P:2 * P], k2[:, :], start=True, stop=True)\
                    .then_inc(tile_full, 1)

            def turn_probs2(h):
                pe.wait_ge(probs2_ready, h + 1)
                if h >= 2:
                    pe.wait_ge(pT2_taken, h - 1)
                b = ps[4 + h % 2]
                for k in range(3):
                    last = transpose(b[:, k * P:(k + 1) * P], probs2[:, h % 3, k * P:(k + 1) * P])
                last.then_inc(pT2_full, 1)

            def weigh_values2(g):
                pe.wait_ge(pT2_taken, HG * (g + 1))
                if g == 0:
                    late_wait(QT + 2 * C)
                    late_wait(QT + 2 * C + 1)
                b = ps[6 + g // 2]
                at = (g % 2) * S
                for k, vt, col, first, final in ((0, 0, 0, True, True), (1, 0, P, True, False),
                                                 (2, 1, P, False, True)):
                    for j in range(HG):
                        h = HG * g + j
                        rows = slice(j * HEAD_DIM, (j + 1) * HEAD_DIM)
                        last = nc.tensor.matmul(b[rows, at + col:at + col + P],
                                                v[:, vt, h * HEAD_DIM:(h + 1) * HEAD_DIM],
                                                pT2[:, h, k * P:(k + 1) * P], start=first, stop=final,
                                                tile_position=(0, j * HEAD_DIM))
                last.then_inc(pv2_full, 1)

            for i in range(H + 3):
                if i < H:
                    scores2(i)
                if 2 <= i < H + 2:
                    turn_probs2(i - 2)
                if i >= 6 and (i - 6) % HG == 0:
                    weigh_values2((i - 6) // HG)
            pe.wait_ge(inv_ready, 2)
            spread(row_inv, inv_spread)
            project(AWO, 2)

            for t in range(QT):
                pe.wait_ge(norm_ready, 2 * QT + t + 1)
                for c in range(C):
                    last = transpose(ps[2 + t][:, c * P:(c + 1) * P], xn[:, t, c * P:(c + 1) * P])
                last.then_inc(tile_full, 1)
            pe.wait_ge(*taken(LATE + NLATE - 2))
            pe.wait_ge(*taken(LATE + NLATE - 1))
            for t in range(QT):
                nc.tensor.matmul(ps[4][:, t * E:(t + 1) * E], ones_row[:, :], rb_row[:, :], start=True, stop=False)
                for c in range(C):
                    last = nc.tensor.matmul(ps[4][:, t * E:(t + 1) * E], xT[:, c, t * P:(t + 1) * P],
                                            rwT[:, c, :], start=False, stop=(c == C - 1))
            last.then_inc(logits_full, 1)

            def expert(n):
                e, t = n // QT, n % QT
                pe.wait_ge(stage_loaded[(8 + e) % NSTAGE], 16 * ((8 + e) // NSTAGE + 1))
                if n >= 4:
                    pe.wait_ge(y_taken, n - 3)
                b = ps[n % 4]
                for c in range(C):
                    last = nc.tensor.matmul(b[:, :], xT[:, c, t * P:(t + 1) * P], stage[:, (8 + e) % NSTAGE, c, :],
                                            start=(c == 0), stop=(c == C - 1))
                last.then_inc(y_full, 1)

            for n in range(4):
                expert(n)
            pe.wait_ge(chosen_ready, 1)
            for t in range(QT):
                last = transpose(ps[5][0:E, t * P:(t + 1) * P], chosen[:, t, :])
            last.then_inc(chosenT_full, 1)
            pe.wait_ge(chosenT_ready, 1)
            for t in range(QT):
                last = nc.tensor.matmul(ps[6 + t][:, :], chosenT[:, t, :], ffn_b_sb[:, :], start=True, stop=True)
            last.then_inc(bias_full, 1)
            for n in range(4, QT * E):
                expert(n)


        @block.scalar
        def _(act):
            for i, b in enumerate((bq, bk, bv)):
                act.dma_start(bias_rows[C * i:C * (i + 1), :], b.rearrange("(c p) -> c p", p=P))\
                    .then_inc(small_loaded, 16)
            act.dma_start(rw_rows[:, :], router_w).then_inc(small_loaded, 16)
            act.dma_start(bf_row[:, :], bf.rearrange("(a d) -> a d", a=1)).then_inc(small_loaded, 16)
            act.dma_start(rb_row[:, :], router_b.rearrange("(a d) -> a d", a=1)).then_inc(small_loaded, 16)
            act.dma_start(ffn_b_sb[:, :], ffn_b).then_inc(small_loaded, 16)

            def layer_norm_root(n):
                act.wait_ge(var_ready, n)
                nc.scalar.activation(ln_rstd[:, :, :], ln_rstd[:, :, :], ACT.Sqrt).then_inc(std_ready, 1)
                if n > 1:
                    load_table(ACT.Exp)

            def load_table(function):
                nc.scalar.activation(table_use[:, loads[0]:loads[0] + 1], ones_row[:, 0:1], function)
                loads[0] += 1

            loads = [0]
            layer_norm_root(1)

            def take_setup(n):
                kind, a = setup_tiles[n]
                act.wait_ge(tile_full, n + 1)
                if kind == "x":
                    dst = xT[:, :, a * P:(a + 1) * P]
                else:
                    w, o = a
                    if w == AWO and o < 2:
                        act.wait_ge(tile_full, q_tile[-1] + 1)
                    dst = wT_high[:, PAIR[w], :, o * P:(o + 1) * P] if w in PAIR else \
                        wT[:, SLOT[w], :, o * P:(o + 1) * P]
                nc.scalar.activation(dst, ps[n % 8][:, :].rearrange("p (c q) -> p c q", c=C), ACT.Copy)\
                    .then_inc(tile_act, 1)

            def scan_group(g):
                act.wait_ge(size_used, ONE + g)
                act.wait_ge(scan_loaded, (g + 1) * 16 * QT)
                for t in range(QT):
                    for i in range(GROUP - ACT_CHUNKS, GROUP):
                        piece = scan_pairs[:, t, i * CHUNK // 2:(i + 1) * CHUNK // 2]
                        last = nc.scalar.activation(piece.bitcast(F32), piece, ACT.Abs,
                                                    accum_out=open_size[:, t, i:i + 1])
                last.then_inc(scan_act, 1)

            for n in range(w_tile[(0, 0)]):
                if takers[n] == "act":
                    take_setup(n)
            for w in range(8):
                for o in range(C):
                    if takers[w_tile[(w, o)]] != "dve":
                        take_setup(w_tile[(w, o)])
                if w == WQ:
                    act.wait_ge(q_full_ready, 1)
                    nc.scalar.activation(q_high, q_full, ACT.Copy).then_inc(q_high_ready, 1)
                if w in EARLY_SCANS:
                    scan_group(EARLY_SCANS[w])
            act.wait_ge(pad_cleared, 1)
            act.wait_ge(q_low_ready, 1)
            for j in range(HG):
                rows = slice(j * HEAD_DIM, (j + 1) * HEAD_DIM)
                nc.scalar.activation(q_pad[rows, j, 0, :], q_high[rows, 0, :], ACT.Copy).then_inc(q_padded, 1)

            def chunk(c, d, scanned):
                for n in range(KT):
                    act.wait_ge(ctx_turned, ONE + d * KT + n + 1)
                    nc.scalar.activation(ctxT_high[:, :, n * P:(n + 1) * P],
                                         ps[n][:, :].rearrange("p (c k) -> p c k", c=C), ACT.Copy)\
                        .then_inc(ring_act, 1)
                def take(kind, n):
                    b = ps[BANK_OF[(kind, n)]]
                    if act_takes((kind, n)):
                        act.wait_ge(*full((kind, n), d))
                        if kind == "k":
                            nc.scalar.activation(kT_high[:, n, :], b[:, :], ACT.Identity,
                                                 bias=bias_cols[:, 1, n:n + 1]).then_inc(ring_act, 1)
                        else:
                            nc.scalar.activation(v[:, n, :], b[:, :], ACT.Copy).then_inc(ring_act, 1)

                if -1 in SCAN_AFTER:
                    scan_one(act, scan_group, scanned)
                take("k", 0)
                take("k", 1)
                for i in range(H + 2):
                    if i < H:
                        act.wait_ge(neg_ready, d * H + i + 1)
                        for t in range(QT):
                            nc.scalar.activation(probs[:, i % 3, t, :], probs[:, i % 3, t, :], ACT.Exp,
                                                 bias=m_neg[:, t, i:i + 1],
                                                 accum_out=chunk_sum[:, t, i:i + 1]).then_inc(probs_ready, 1)
                    if i in BETWEEN:
                        take(*BETWEEN[i][:2])
                    if i == H:
                        act.wait_ge(diff_ready, d + 1)
                        nc.scalar.activation(alpha[:, :, :], m_diff[:, :, :], ACT.Exp).then_inc(alpha_ready, 1)
                    if i >= 2:
                        h = i - 2
                        act.wait_ge(pT_full, ONE + d * QT * H + QT * h + 1)
                        if h >= TURNED:
                            act.wait_ge(pv_full, d * C + (h - TURNED) // HG + 1)
                        nc.scalar.activation(pT[:, h % TURNED, :, 0:P],
                                             ps[2 + QT * h % 4][:, :].rearrange("p (k q) -> p k q", k=KT),
                                             ACT.Copy).then_inc(pT_act, 1)
                    if i in SCAN_AFTER:
                        scan_one(act, scan_group, scanned)

            open_chunks(act, chunk, scan_group)

            load_table(ACT.Sqrt)
            layer_norm_root(2)
            for t in range(QT):
                act.wait_ge(tile_full, LATE + t + 1)
                nc.scalar.activation(xT_high[:, :, t * P:(t + 1) * P],
                                     ps[t][:, :].rearrange("p (c q) -> p c q", c=C), ACT.Copy).then_inc(tile_act, 1)
            act.wait_ge(zeros_ready, 1)
            for g in (0, 2):
                n = QT + g
                act.wait_ge(tile_full, LATE + n + 1)
                for j in range(HG):
                    rows = slice(j * HEAD_DIM, (j + 1) * HEAD_DIM)
                    last = nc.scalar.activation(q2_pad[rows, HG * g + j, :], ps[n % RING][rows, 0:S], ACT.Copy,
                                                scale=SCALE)
                last.then_inc(tile_act, 1)
            for g in (0, 2):
                n = QT + C + g
                act.wait_ge(tile_full, LATE + n + 1)
                nc.scalar.activation(k2T[:, g, :], ps[n % RING][:, 0:S], ACT.Copy).then_inc(tile_act, 1)
            n = QT + 2 * C
            act.wait_ge(tile_full, LATE + n + 1)
            nc.scalar.activation(v[:, 0, :], ps[n % RING][:, :], ACT.Copy).then_inc(tile_act, 1)
            for h in range(H):
                act.wait_ge(neg2_ready, h + 1)
                nc.scalar.activation(probs2[:, h % 3, 0:P], probs2[:, h % 3, 0:P], ACT.Exp,
                                     bias=m_neg[:, 0, h:h + 1], accum_out=row_sum[:, 0, h:h + 1])
                nc.scalar.activation(probs2[:, h % 3, P:], probs2[:, h % 3, P:], ACT.Exp,
                                     bias=m_neg[:, 1, h:h + 1], accum_out=row_sum[:, 1, h:h + 1])\
                    .then_inc(probs2_ready, 1)

            load_table(ACT.Sqrt)
            layer_norm_root(3)
            act.wait_ge(tile_full, LATE + NLATE - 1)
            nc.scalar.activation(xT[:, :, 0:P], ps[2][:, :].rearrange("p (c q) -> p c q", c=C), ACT.Copy)\
                .then_inc(tile_act, 1)
            act.wait_ge(shift_ready, 1)
            nc.scalar.activation(score[:, :, :], logit[:, :, :], ACT.Exp).then_inc(exp_ready, 1)
            act.wait_ge(chosenT_full, 1)
            nc.scalar.activation(chosenT[:, :, :], ps[5][0:E, 0:QT * P].rearrange("e (t q) -> e t q", t=QT), ACT.Copy)\
                .then_inc(chosenT_ready, 1)

        @block.vector
        def _(dve):
            steps = [0]
            norms = [0]

            def link(ins):
                steps[0] += 1
                ins.then_inc(dve_step, 1)
                dve.wait_ge(dve_step, steps[0])

            def layer_norm():
                for t in range(QT):
                    last = nc.vector.bn_stats(ln_stats[:, t, :], res[:, t, :])
                link(last)
                for t in range(QT):
                    last = nc.vector.bn_aggr(ln_mv[:, t, :], ln_stats[:, t, :])
                link(last)
                nc.vector.tensor_scalar(ln_rstd[:, :, :], ln_mv[:, :, 1:2], LN_EPS, None, ALU.add)\
                    .then_inc(var_ready, 1)
                norms[0] += 1
                dve.wait_ge(std_ready, norms[0])
                link(nc.vector.reciprocal(ln_rstd[:, :, :], ln_rstd[:, :, :]))
                for t in range(QT):
                    nc.vector.tensor_scalar(xn[:, t, :], res[:, t, :], ln_mv[:, t, 0:1], ln_rstd[:, t, :],
                                            ALU.subtract, ALU.mult).then_inc(norm_ready, 1)

            def take_setup(n):
                kind, a = setup_tiles[n]
                dve.wait_ge(tile_full, n + 1)
                b = ps[n % 8]
                quarters = b[:, :].rearrange("p (c q) -> p c q", c=C)
                if kind == "x":
                    last = nc.vector.tensor_copy(xT[:, :, a * P:(a + 1) * P], quarters)
                elif kind == "w":
                    w, o = a
                    if w in PAIR:
                        dve.wait_ge(tile_act, act_took(n))
                        last = nc.vector.tensor_tensor(wT_low[:, PAIR[w], :, o * P:(o + 1) * P], quarters,
                                                       wT_high[:, PAIR[w], :, o * P:(o + 1) * P], ALU.subtract)
                    else:
                        last = nc.vector.tensor_copy(wT[:, SLOT[w], :, o * P:(o + 1) * P], quarters)
                elif kind == "small":
                    link(nc.vector.tensor_copy(bias_cols[:, :, :], b[:, 0:3 * C].rearrange("p (i c) -> p i c", i=3)))
                    last = nc.vector.tensor_copy(rwT[:, :, :], b[:, 64:64 + C * E].rearrange("p (c e) -> p c e", c=C))
                else:
                    last = nc.vector.tensor_scalar(q_full[:, a, :], b[:, 0:S], bias_cols[:, 0, a:a + 1], SCALE,
                                                   ALU.add, ALU.mult)
                last.then_inc(tile_dve, 1)

            def scan_group(g):
                n = GROUP - ACT_CHUNKS
                dve.wait_ge(size_used, ONE + g)
                dve.wait_ge(scan_loaded, (g + 1) * 16 * QT)
                for t in range(QT):
                    last = nc.vector.tensor_reduce(open_size[:, t, 0:n],
                                                   scan_pairs[:, t, 0:n * CHUNK // 2].rearrange("p (c k) -> p c k", c=n),
                                                   AX.X, ALU.max, apply_absolute_value=True)
                last.then_inc(scan_dve, 1)

            for starts_at_one in (mask_used, ring_dve, fold_step):
                dve.sem_inc(starts_at_one, ONE)
            dve.wait_ge(x_loaded, 16)
            layer_norm()
            for n in range(3):
                if takers[n] == "dve":
                    take_setup(n)
            for w in range(8):
                for o in range(C):
                    if takers[w_tile[(w, o)]] != "act":
                        take_setup(w_tile[(w, o)])
                if w == WQ:
                    for n in q_tile:
                        take_setup(n)
                    dve.wait_ge(*taken(q_tile[-1]))
                    dve.sem_inc(q_full_ready, 1)
                    dve.wait_ge(q_high_ready, 1)
                    nc.vector.tensor_tensor(q_low, q_full, q_high, ALU.subtract).then_inc(q_low_ready, 1)
                if w in EARLY_SCANS:
                    scan_group(EARLY_SCANS[w])

            dve.wait_ge(pad_cleared, 1)
            dve.wait_ge(q_low_ready, 1)
            for j in range(HG):
                rows = slice(j * HEAD_DIM, (j + 1) * HEAD_DIM)
                nc.vector.tensor_copy(q_pad[rows, j, 1, :], q_low[rows, 0, :]).then_inc(q_padded, 1)

            def chunk(c, d, scanned):
                fold = [0]

                def fold_link(ins):
                    fold[0] += 1
                    ins.then_inc(fold_step, 1)
                    dve.wait_ge(fold_step, ONE + d * FOLD + fold[0])

                for n in range(KT):
                    dve.wait_ge(ring_act, d * RING_ACT + n + 1)
                    nc.vector.tensor_tensor(ctxT_low[:, :, n * P:(n + 1) * P],
                                            ps[n][:, :].rearrange("p (c k) -> p c k", c=C),
                                            ctxT_high[:, :, n * P:(n + 1) * P], ALU.subtract).then_inc(ring_dve, 1)
                dve.wait_ge(mask_loaded, d * 16 + 16)
                fold_link(nc.vector.tensor_scalar(mask_add[:, :, :], mask_in[:, :, :], 0.0, MASKED,
                                                  ALU.is_equal, ALU.mult))
                dve.sem_inc(mask_used, 1)

                def take(kind, n):
                    b = ps[BANK_OF[(kind, n)]]
                    if kind == "k":
                        dve.wait_ge(*by_act((kind, n), d))
                        nc.vector.scalar_tensor_tensor(out=kT_low[:, n, :], in0=b[:, :],
                                                       scalar=bias_cols[:, 1, n:n + 1], in1=kT_high[:, n, :],
                                                       op0=ALU.add, op1=ALU.subtract).then_inc(ring_dve, 1)
                    elif dve_takes((kind, n)):
                        dve.wait_ge(*full((kind, n), d))
                        nc.vector.tensor_copy(v[:, n, :], b[:, :]).then_inc(ring_dve, 1)

                if -1 in SCAN_AFTER:
                    scan_one(dve, scan_group, scanned)
                take("k", 0)
                take("k", 1)
                for i in range(H + 2):
                    if i < H:
                        if i >= 3:
                            dve.wait_ge(pT_full, ONE + d * QT * H + QT * (i - 2))
                        else:
                            dve.wait_ge(pT_full, ONE + d * QT * H)
                        for t in range(QT):
                            dve.wait_ge(*full(("score", QT * i + t), d))
                            nc.vector.memset(gate[:, t, i:i + 1], 0.0)
                            nc.vector.tensor_tensor_reduce(probs[:, i % 3, t, :], ps[t][:, :], mask_add[:, t, :],
                                                           1.0, m_run[:, t, i:i + 1], ALU.add, ALU.max,
                                                           m_new[:, t, i:i + 1]).then_inc(ring_dve, 1)
                        dve.wait_ge(*by_dve(("score", QT * i + 1), d))
                        nc.vector.tensor_scalar(m_neg[:, :, i:i + 1], m_new[:, :, i:i + 1], -1.0, None, ALU.mult)\
                            .then_inc(neg_ready, 1)
                        if i - 1 in BETWEEN:
                            take(*BETWEEN[i - 1][:2])
                    if i == H - 1:
                        fold_link(nc.vector.tensor_tensor(m_diff[:, :, :], m_run[:, :, :], m_new[:, :, :],
                                                          ALU.subtract))
                        dve.sem_inc(diff_ready, 1)
                    if i >= 2:
                        h = i - 2
                        dve.wait_ge(pT_full, ONE + d * QT * H + QT * h + 2)
                        if h >= TURNED:
                            dve.wait_ge(pv_full, d * C + (h - TURNED) // HG + 1)
                        nc.vector.tensor_copy(pT[:, h % TURNED, :, P:2 * P],
                                              ps[2 + (QT * h + 1) % 4][:, :]
                                              .rearrange("p (k q) -> p k q", k=KT)).then_inc(pT_dve, 1)
                    if i in SCAN_AFTER:
                        scan_one(dve, scan_group, scanned)
                dve.wait_ge(probs_ready, (d + 1) * QT * H)
                dve.wait_ge(alpha_ready, d + 1)
                fold_link(nc.vector.tensor_tensor(row_sum[:, :, :], row_sum[:, :, :], alpha[:, :, :], ALU.mult))
                fold_link(nc.vector.tensor_tensor(row_sum[:, :, :], row_sum[:, :, :], chunk_sum[:, :, :], ALU.add))
                fold_link(nc.vector.tensor_copy(m_run[:, :, :], m_new[:, :, :]))
                halves = [oT[:, 2 * b:2 * b + 2, :].rearrange("p g q -> p (g q)") for b in range(2)]
                for b, half in enumerate(halves):
                    dve.wait_ge(alpha_spread, d * 2 + b + 1)
                    fold_link(nc.vector.tensor_tensor(half, half, ps[4 + b][:, :], ALU.mult))
                for b, half in enumerate(halves):
                    dve.wait_ge(pv_full, d * C + 2 * (b + 1))
                    fold_link(nc.vector.tensor_tensor(half, half, ps[6 + b][:, :], ALU.add))
                assert fold[0] == FOLD

            open_chunks(dve, chunk, scan_group)

            def invert_sums():
                nc.vector.reciprocal(row_inv[:, :, :], row_sum[:, :, :]).then_inc(inv_ready, 1)

            invert_sums()
            for b in range(2):
                dve.wait_ge(inv_spread, b + 1)
                half = oT[:, 2 * b:2 * b + 2, :].rearrange("p g q -> p (g q)")
                link(nc.vector.tensor_tensor(half, half, ps[4 + b][:, :], ALU.mult))
                for g in (2 * b, 2 * b + 1):
                    link(nc.vector.tensor_scalar(oT[:, g, :], oT[:, g, :], bias_cols[:, 2, g:g + 1], None, ALU.add))
                dve.sem_inc(oT_ready, 1)

            def add_projection(n):
                for t in range(QT):
                    dve.wait_ge(proj_full, QT * n + t + 1)
                    link(nc.vector.tensor_tensor(res[:, t, :], res[:, t, :], ps[t][:, :], ALU.add))

            add_projection(0)
            layer_norm()

            def late_wait(n):
                dve.wait_ge(tile_full, LATE + n + 1)
                return ps[n % RING]

            for t in range(QT):
                b = late_wait(t)
                dve.wait_ge(tile_act, act_took(LATE + t))
                nc.vector.tensor_tensor(xT_low[:, :, t * P:(t + 1) * P], b[:, :].rearrange("p (c q) -> p c q", c=C),
                                        xT_high[:, :, t * P:(t + 1) * P], ALU.subtract).then_inc(tile_dve, 1)
            dve.wait_ge(zeros_ready, 1)
            for g in (1, 3):
                b = late_wait(QT + g)
                for j in range(HG):
                    rows = slice(j * HEAD_DIM, (j + 1) * HEAD_DIM)
                    last = nc.vector.tensor_scalar(q2_pad[rows, HG * g + j, :], b[rows, 0:S], SCALE, None, ALU.mult)
                last.then_inc(tile_dve, 1)
            for g in (1, 3):
                b = late_wait(QT + C + g)
                nc.vector.tensor_copy(k2T[:, g, :], b[:, 0:S]).then_inc(tile_dve, 1)
            b = late_wait(QT + 2 * C + 1)
            nc.vector.tensor_copy(v[:, 1, :], b[:, :]).then_inc(tile_dve, 1)
            for i in range(H + 2):
                if i < H:
                    b = late_wait(2 * QT + 2 * C + i)
                    if i >= 3:
                        dve.wait_ge(pT2_full, i - 2)
                    p2 = probs2[:, i % 3, :]
                    nc.vector.tensor_tensor_reduce(p2[:, 0:P], b[:, 0:P], window[:, P:], 1.0, LOWEST,
                                                   ALU.add, ALU.max, m_new[:, 0, i:i + 1])
                    nc.vector.tensor_tensor_reduce(p2[:, P:], b[:, P:3 * P], window[:, :], 1.0, LOWEST,
                                                   ALU.add, ALU.max, m_new[:, 1, i:i + 1]).then_inc(tile_dve, 1)
                    dve.wait_ge(*taken(LATE + 2 * QT + 2 * C + i))
                    nc.vector.tensor_scalar(m_neg[:, :, i:i + 1], m_new[:, :, i:i + 1], -1.0, None, ALU.mult)\
                        .then_inc(neg2_ready, 1)
                if i >= 2:
                    h = i - 2
                    dve.wait_ge(pT2_full, h + 1)
                    nc.vector.tensor_copy(pT2[:, h, :], ps[4 + h % 2][:, 0:3 * P]).then_inc(pT2_taken, 1)
            dve.wait_ge(probs2_ready, H)
            invert_sums()
            for g in range(2):
                dve.wait_ge(pv2_full, 2 * g + 2)
                half = oT[:, 2 * g:2 * g + 2, :].rearrange("p g q -> p (g q)")
                link(nc.vector.tensor_copy(half, ps[6 + g][:, :]))
                dve.wait_ge(inv_spread, 2 + g + 1)
                link(nc.vector.tensor_tensor(half, half, ps[4 + g][:, :], ALU.mult))
                dve.sem_inc(oT_ready, 1)
            add_projection(1)
            layer_norm()

            dve.wait_ge(tile_full, LATE + NLATE)
            nc.vector.tensor_copy(xT[:, :, P:2 * P], ps[3][:, :].rearrange("p (c q) -> p c q", c=C))\
                .then_inc(tile_dve, 1)
            dve.wait_ge(logits_full, 1)
            logits = ps[4][:, 0:QT * E].rearrange("p (t e) -> p t e", t=QT)
            link(nc.vector.tensor_reduce(r_max[:, :, :], logits, AX.X, ALU.max))
            link(nc.vector.tensor_tensor(logit[:, :, :], logits, r_max[:, :, :].broadcast_to([P, QT, E]),
                                         ALU.subtract))
            dve.sem_inc(shift_ready, 1)
            dve.wait_ge(exp_ready, 1)
            link(nc.vector.tensor_reduce(r_sum[:, :, :], score[:, :, :], AX.X, ALU.add))
            link(nc.vector.reciprocal(r_inv[:, :, :], r_sum[:, :, :]))
            link(nc.vector.tensor_tensor(score[:, :, :], score[:, :, :], r_inv[:, :, :].broadcast_to([P, QT, E]),
                                         ALU.mult))
            for t in range(QT):
                other = score[:, t, :].unsqueeze(1).broadcast_to([P, E, E])
                own = score[:, t, :].unsqueeze(2).broadcast_to([P, E, E])
                nc.vector.tensor_tensor(above[:, t, :, :], other, own, ALU.is_gt)
                link(nc.vector.tensor_tensor(tied[:, t, :, :], other, own, ALU.is_equal))
                link(nc.vector.tensor_tensor(tied[:, t, :, :], tied[:, t, :, :], lower[:, :, :], ALU.mult))
                link(nc.vector.tensor_tensor(above[:, t, :, :], above[:, t, :, :], tied[:, t, :, :], ALU.add))
            link(nc.vector.tensor_reduce(rank[:, :, :], above[:, :, :, :], AX.X, ALU.add))
            link(nc.vector.tensor_scalar(chosen[:, :, :], rank[:, :, :], TOP_K - 0.5, None, ALU.is_lt))
            dve.sem_inc(chosen_ready, 1)

            dve.wait_ge(bias_full, 1)
            for t in range(QT):
                link(nc.vector.tensor_tensor(res[:, t, :], res[:, t, :], ps[6 + t][:, :], ALU.add))
            for n in range(QT * E):
                e, t = n // QT, n % QT
                dve.wait_ge(y_full, n + 1)
                if n >= QT:
                    dve.wait_ge(y_taken, n - QT + 1)
                nc.vector.scalar_tensor_tensor(out=res[:, t, :], in0=ps[n % 4][:, :], scalar=chosen[:, t, e:e + 1],
                                               in1=res[:, t, :], op0=ALU.mult, op1=ALU.add)\
                    .then_inc(y_taken, 1)
            for t in range(QT):
                dve.wait_ge(y_taken, QT * (E - 1) + t + 1)
                dve.sem_inc(out_ready, 1)


_INS = ['x', 'ctx_1024', 'mask_1x1xSxS2_ik0', 'L0_xattn_Wq', 'L0_xattn_bq', 'L0_xattn_Wk', 'L0_xattn_bk',
        'L0_xattn_Wv', 'L0_xattn_bv', 'L0_xattn_Wf', 'L0_xattn_bf', 'L0_attn_Wq', 'L0_attn_Wk', 'L0_attn_Wv',
        'L0_attn_Wo', 'L0_ffn_weight', 'L0_ffn_bias', 'L0_ffn_router_weight', 'L0_ffn_router_bias']


def kernel(**inputs):
    import numpy as np
    import concourse.bacc as bacc
    from concourse.bass_utils import run_bass_kernel_spmd

    nc = bacc.Bacc("TRN2", target_bir_lowering=False, num_devices=1)
    arrays, args = {}, []
    for name in _INS:
        a = np.ascontiguousarray(inputs[name])
        arrays[f"in_{name}"] = a
        args.append(nc.dram_tensor(f"in_{name}", a.shape, mybir.dt.from_np(a.dtype), kind="ExternalInput").ap())
    out = nc.dram_tensor("out_x", inputs['x'].shape, F32, kind="ExternalOutput").ap()
    build_perceiver(nc, *args, out)
    r = run_bass_kernel_spmd(nc, [arrays], core_ids=[0])
    return r.results[0]["out_x"]
```
